# Optimizing a Trainium2 kernel written in Bass

```python
import numpy as np
import jax
import jax.numpy as jnp

def _softmax(x, axis=-1):
    return jax.nn.softmax(x, axis=axis)

def _gelu(x):
    return jax.nn.gelu(x, approximate=True)

def _silu(x):
    return jax.nn.silu(x)

def _sigmoid(x):
    return jax.nn.sigmoid(x)

def _layernorm(x, axis=-1, eps=1e-05):
    m = jnp.mean(x, axis=axis, keepdims=True)
    v = jnp.var(x, axis=axis, keepdims=True)
    return (x - m) / jnp.sqrt(v + eps)

def _scatter_add(tgt, idx, src, axis=0):
    return tgt.at[idx].add(src)

def _segment_sum(src, seg, n):
    return jax.ops.segment_sum(src, seg, n)
kernel_name = 'mk_adj_preln_d2_adj_r2_7977ea'

def setup_inputs(seed: int=0):
    np.random.seed(seed)
    _w = jnp.asarray

    def _rec_inputs():
        import jax
        import jax.numpy as jnp
        _gk = jax.random.key(seed)
        x = -0.0005207 + 1.001 * jax.random.normal(jax.random.fold_in(_gk, 1), (8192, 128), jnp.float32)
        _a = jax.random.bernoulli(jax.random.fold_in(_gk, 2), 0.000976562, (8192, 8192))
        adj = _a.astype(jnp.int32)
        return (x, adj)
    x, adj = _rec_inputs()

    def _L0_gnn_setup():
        import jax, jax.numpy as jnp
        import numpy as np
        N, D, H = (4096, 128, 128)
        KEEP_RATIO = 0.5
        TEMP = 1.0
        COS_EPS = 0.0001
        NEG = -9000000000000000.0

        def _cos_normalize(x):
            n = jnp.linalg.norm(x, axis=-1, keepdims=True)
            return x / jnp.maximum(n, COS_EPS)
        key = jax.random.key(seed)
        k1, k2, k3, k4 = jax.random.split(key, 4)
        features = jax.random.normal(k1, (N, D), dtype=jnp.float32)
        adj = jax.random.randint(k2, (N, N), 0, 2, dtype=jnp.int32)
        Wq = jax.random.normal(k3, (H, D), dtype=jnp.float32) * 0.001
        Wk = jax.random.normal(k4, (H, D), dtype=jnp.float32) * 0.001
        return {'features': features, 'adj': adj, 'Wq': Wq, 'Wk': Wk}
    _L0_gnn_all = _L0_gnn_setup()
    _L0_gnn_in = {k: v for k, v in _L0_gnn_all.items() if k in ('Wq', 'Wk')}
    del _L0_gnn_all

    def _L1_gnn_setup():
        import jax, jax.numpy as jnp
        import numpy as np
        N = 4096
        D_IN = 128
        D_OUT = 128
        NEG_INF = -9000000000000000.0
        key = jax.random.key(seed)
        k1, k2, k3, k4 = jax.random.split(key, 4)
        node_features = jax.random.normal(k1, (N, D_IN), dtype=jnp.float32)
        adjacency_matrix = jax.random.randint(k2, (N, N), 0, 2, dtype=jnp.int32)
        W = jax.random.normal(k3, (D_OUT, D_IN), dtype=jnp.float32) / np.sqrt(D_IN)
        b_W = jnp.zeros((D_OUT,), dtype=jnp.float32)
        a_vec = jax.random.normal(k4, (2 * D_OUT,), dtype=jnp.float32) / np.sqrt(2 * D_OUT)
        b_a = jnp.zeros((1,), dtype=jnp.float32)
        return {'node_features': node_features, 'adjacency_matrix': adjacency_matrix, 'W': W, 'b_W': b_W, 'a_vec': a_vec, 'b_a': b_a}
    _L1_gnn_all = _L1_gnn_setup()
    _L1_gnn_in = {k: v for k, v in _L1_gnn_all.items() if k in ('W', 'b_W', 'a_vec', 'b_a')}
    del _L1_gnn_all
    return {'x': x, 'adj': adj, 'L0_gnn_Wq': _L0_gnn_in['Wq'], 'L0_gnn_Wk': _L0_gnn_in['Wk'], 'L1_gnn_W': _L1_gnn_in['W'], 'L1_gnn_b_W': _L1_gnn_in['b_W'], 'L1_gnn_a_vec': _L1_gnn_in['a_vec'], 'L1_gnn_b_a': _L1_gnn_in['b_a']}

def reference(x, adj, L0_gnn_Wq, L0_gnn_Wk, L1_gnn_W, L1_gnn_b_W, L1_gnn_a_vec, L1_gnn_b_a):
    import jax
    import jax.numpy as jnp

    def _L0_gnn_ref(features, adj, Wq, Wk):
        import jax, jax.numpy as jnp
        import numpy as np
        N, D, H = (4096, 128, 128)
        KEEP_RATIO = 0.5
        TEMP = 1.0
        COS_EPS = 0.0001
        NEG = -9000000000000000.0

        def _cos_normalize(x):
            n = jnp.linalg.norm(x, axis=-1, keepdims=True)
            return x / jnp.maximum(n, COS_EPS)
        Qn = _cos_normalize(features @ Wq.T)
        Kn = _cos_normalize(features @ Wk.T)
        raw_att = Kn @ Qn.T
        att = jnp.where(adj > 0, raw_att, NEG) * TEMP
        att = jax.nn.softmax(att, axis=1)
        prop_fea = att @ features
        adj_mask = (jnp.sum(adj, axis=1) > 0).astype(features.dtype)[:, None]
        prop_fea = adj_mask * prop_fea + (1.0 - adj_mask) * features
        return (1.0 - KEEP_RATIO) * prop_fea + KEEP_RATIO * features

    def _L1_gnn_ref(node_features, adjacency_matrix, W, b_W, a_vec, b_a):
        import jax, jax.numpy as jnp
        import numpy as np
        N = 4096
        D_IN = 128
        D_OUT = 128
        NEG_INF = -9000000000000000.0
        h = node_features @ W.T + b_W
        a1, a2 = (a_vec[:D_OUT], a_vec[D_OUT:])
        e = (h @ a1)[:, None] + (h @ a2)[None, :] + b_a[0]
        e = jnp.where(e > 0, e, 0.2 * e)
        scores = jnp.where(adjacency_matrix > 0, e, jnp.float32(NEG_INF))
        attention = jax.nn.softmax(scores, axis=1)
        h_prime = attention @ h
        return h_prime
    h = jnp.maximum(_layernorm(x, axis=-1), 0.0)
    x = x + _L0_gnn_ref(h, adj, L0_gnn_Wq, L0_gnn_Wk)
    h = jnp.maximum(_layernorm(x, axis=-1), 0.0)
    x = x + _L1_gnn_ref(h, adj, L1_gnn_W, L1_gnn_b_W, L1_gnn_a_vec, L1_gnn_b_a)
    return x

_drawn_inputs = setup_inputs


def setup_inputs(seed=0):
    import zlib

    import numpy as np

    out = dict(_drawn_inputs(seed))
    spreads = {'L1_gnn_b_W': (0.0, 0.1)}
    factors = {}
    for name, (base, spread) in spreads.items():
        noise = np.random.default_rng([zlib.crc32(name.encode()), seed]).standard_normal(out[name].shape)
        drawn = base * np.exp(spread * noise) if base else spread * noise
        out[name] = jnp.asarray(drawn.astype(out[name].dtype))
    for name, factor in factors.items():
        out[name] = (out[name] * factor).astype(out[name].dtype)
    return out
```

```python
import concourse.bass as bass
from concourse import mybir
from contextlib import ExitStack


class Chain:

    def __init__(self, eng, sem):
        self.eng, self.sem, self.at, self.n = eng, sem, 0, 0

    def __call__(self, instruction, gate=None):
        self.n += 1
        instruction.then_inc(self.sem, 1)
        self.eng.wait_ge(self.sem, self.at + self.n)
        if gate is not None:
            self.eng.sem_inc(gate, 1)

    def loop(self, i, first, per):
        self.start, self.first, self.per = self.at + self.n, first, per
        self.at, self.n = self.start + (i - first) * per, 0

    def ended(self, end):
        assert self.n == self.per, (self.n, self.per)
        self.at, self.n = self.start + (end - self.first) * self.per, 0


def peel(eng, link, first, end, body):
    before = link.n if link else 0
    body(first, True)
    per = link.n - before if link else 0
    with eng.Fori(first + 1, end) as i:
        if link:
            link.loop(i, first + 1, per)
        body(i, False)
    if link:
        link.ended(end)


def adjacency_layers(nc, x, adj, wq, wk, w, b_w, a_vec, b_a, out):
    fp32, bf16, i32 = mybir.dt.float32, mybir.dt.bfloat16, mybir.dt.int32
    ALU, ACT, AX = mybir.AluOpType, mybir.ActivationFunctionType, mybir.AxisListType

    N, D = x.shape
    P = 128
    T = N // P
    TB = 8
    NB = T // TB
    S = 24
    S0 = 8
    ROUNDS = 3
    BITS, SHIFT = 14, 10
    WORDS = -(-N // BITS)
    HW = WORDS // 2
    LAST = N - (BITS - 1) * WORDS
    CUT = BITS // 2 * WORDS
    assert WORDS % 2 == 0 and WORDS <= 1 << SHIFT and BITS + SHIFT <= 24
    EXP0 = 127 + SHIFT
    NONE = 8192
    assert N == NONE
    FAR_IDX = float(1 << 20)
    EPS, COS_EPS, LEAK, KEEP = 1e-5, 1e-4, 0.2, 0.5
    FAR = 3e38
    WA = D + 2

    qh_tab = nc.dram_tensor("qh_tab", (N, 2 * D), fp32).ap()
    kh_tab = nc.dram_tensor("kh_tab", (N, 2 * D), fp32).ap()
    hw_tab = nc.dram_tensor("hw_tab", (N, WA), fp32).ap()
    qh_b = qh_tab.rearrange("(b s p) c -> b p s c", p=P, s=TB)
    kh_b = kh_tab.rearrange("(b s p) c -> b p s c", p=P, s=TB)
    hw_b = hw_tab.rearrange("(b s p) c -> b p s c", p=P, s=TB)
    qh_t = qh_tab.rearrange("(t p) c -> t p c", p=P)
    kh_t = kh_tab.rearrange("(t p) c -> t p c", p=P)
    hw_t = hw_tab.rearrange("(t p) c -> t p c", p=P)
    adj_t = adj.rearrange("(t p) c -> t p c", p=P)
    out_t = out.rearrange("(t p) c -> t p c", p=P)

    ctx = ExitStack()
    with ctx:
        def sb(name, shape, dt=fp32):
            return ctx.enter_context(nc.sbuf_tensor(name, shape, dt))

        def sem(name):
            return ctx.enter_context(nc.semaphore(name))

        ident = sb("ident", [P, P])
        ident16 = sb("ident16", [P, P], bf16)
        ones = sb("ones", [P, P])
        ones16 = sb("ones16", [1, P], bf16)
        fold = sb("fold", [P, BITS, P], bf16)
        w_hi = sb("w_hi", [1, 19 * 32], bf16)
        w_lo = sb("w_lo", [1, 19 * 32], bf16)
        wqkT = sb("wqkT", [P, 2 * D])
        wa = sb("wa", [P, WA])
        ba = sb("ba", [1, WA])
        wraw = sb("wraw", [P, 3 * D])
        avec = sb("avec", [P, 2])
        bcol = sb("bcol", [P, 1])
        brow = sb("brow", [1, D + 1])
        res = sb("res", [P, T, D])
        idx_all = sb("idx_all", [P, T * S], i32)
        cnt_all = sb("cnt_all", [P, T])
        deg_all = sb("deg_all", [P, 2 * T])
        kmax_all = sb("kmax_all", [1, T], i32)
        goal_all = sb("goal_all", [1, T], i32)
        kput = sb("kput", [1, 2])
        ksum = sb("ksum", [1, 2])
        s1_all = sb("s1_all", [P, T])
        colsum = sb("colsum", [P, D])
        meanb = sb("meanb", [P, D])
        flag = sb("flag", [1, 1], i32)
        small = sb("small", [P, 64])

        G_W = S * (WA + D)
        assert G_W >= S * 2 * D

        arena = sb("arena", [P, 2 * N + N // 2 + 16 + 2 * G_W + 12 * D])

        pos = [0]

        def take(n):
            n += n % 2
            pos[0] += n
            return arena[:, pos[0] - n:pos[0]]

        xc = take(TB * D).rearrange("p (s c) -> p s c", s=TB)
        sq = take(2 * TB * D).rearrange("p (s c) -> p s c", s=2 * TB)
        hb = take(TB * D).rearrange("p (s c) -> p s c", s=TB)
        hT = take(TB * D).rearrange("p (s c) -> p s c", s=TB)
        qk = take(2 * TB * D).rearrange("p (s c) -> p s c", s=TB)
        tw = take(TB * WA).rearrange("p (s c) -> p s c", s=TB)
        pos[0] = 0
        adj_sb = [[take(CUT).bitcast(i32), take(N - CUT).bitcast(i32)] for _ in range(2)]
        m16 = [take(CUT // 2).bitcast(bf16)[:, 0:CUT], take((N - CUT) // 2).bitcast(bf16)[:, 0:N - CUT]]
        G = [take(G_W) for _ in range(2)]
        own = [take(2 * D) for _ in range(2)]
        outb = [take(D) for _ in range(2)]
        G0 = [g[:, 0:S * 2 * D].rearrange("p (s c) -> p s c", s=S) for g in G]
        G1 = [g[:, 0:S * WA].rearrange("p (s c) -> p s c", s=S) for g in G]
        diag1 = [g[:, S * WA:S * (WA + D)].rearrange("p (s c) -> p s c", s=S) for g in G]
        idx_st = [sb(f"idx_st{p}", [P, S], i32) for p in range(2)]
        top = sb("top", [P, 2, S])
        keys = sb("keys", [P, 2, HW])
        wpos = sb("wpos", [P, 2, S])
        left = sb("left", [P, 2, S])
        tbit = sb("tbit", [P, 2, S], i32)
        expo = sb("expo", [P, 2, S], i32)
        cnt2 = sb("cnt2", [P, 2])
        cand = sb("cand", [P, 2, ROUNDS, S])
        nbr = sb("nbr", [P, 2, S])
        valid = sb("valid", [P, 2, S])
        score = sb("score", [P, 2, S])
        prob = sb("prob", [P, 2, S])
        negm = sb("negm", [P, 2, S])
        st = sb("st", [P, 32])

        ps = [ctx.enter_context(nc.psum_tensor(f"ps{i}", [P, 512], fp32)) for i in range(8)]

        s_w, s_x, s_const = sem("weights_loaded"), sem("x_loaded"), sem("constants_made")
        s_wt, s_cpool, s_cdve = sem("weights_transposed"), sem("const_pool_chain"), sem("const_dve_chain")
        with nc.Block() as block:
            @block.sync
            def _(sp):
                sp.dma_start(wraw[:, 0:D], wq).then_inc(s_w, 16)
                sp.dma_start(wraw[:, D:2 * D], wk).then_inc(s_w, 16)
                sp.dma_start(wraw[:, 2 * D:3 * D], w).then_inc(s_w, 16)
                sp.dma_start(avec[:, 0:1], a_vec[D:2 * D].rearrange("(p o) -> p o", o=1)).then_inc(s_w, 16)
                sp.dma_start(avec[:, 1:2], a_vec[0:D].rearrange("(p o) -> p o", o=1)).then_inc(s_w, 16)
                sp.dma_start(bcol[:, :], b_w.rearrange("(p o) -> p o", o=1)).then_inc(s_w, 16)
                sp.dma_start(brow[:, 0:D], b_w.rearrange("(o p) -> o p", o=1)).then_inc(s_w, 16)
                sp.dma_start(brow[:, D:D + 1], b_a.rearrange("(o p) -> o p", o=1)).then_inc(s_w, 16)
                x_t = x.rearrange("(t p) c -> p t c", p=P)
                for b in range(NB):
                    sp.dma_start(res[:, b * TB:(b + 1) * TB, :], x_t[:, b * TB:(b + 1) * TB, :]).then_inc(s_x, 16)
                sp.wait_ge(s_x, 16 * NB)

            @block.gpsimd
            def _(pool):
                link = Chain(pool, s_cpool)
                link(nc.gpsimd.memset(ident[:, :], 0.0))
                link(nc.gpsimd.affine_select(out=ident[:, :], in_=ident[:, :], compare_op=ALU.not_equal,
                                             fill=1.0, base=0, pattern=[[-1, P]], channel_multiplier=1))
                link(nc.gpsimd.memset(ones[:, :], 1.0))
                link(nc.gpsimd.memset(ones16[:, :], 1.0))
                link(nc.gpsimd.iota(w_hi[:, :], [[32, 19], [0, 32]], base=0, channel_multiplier=0,
                                    allow_small_or_imprecise_dtypes=True))
                nc.gpsimd.iota(w_lo[:, :], [[0, 19], [1, 32]], base=0, channel_multiplier=0,
                               allow_small_or_imprecise_dtypes=True).then_inc(s_const, 1)

            @block.tensor
            def _(pe):
                pe.wait_ge(s_w, 128)
                pe.wait_ge(s_const, 1)
                for k in range(3):
                    nc.tensor.transpose(ps[0][:, k * D:(k + 1) * D], wraw[:, k * D:(k + 1) * D], ident[:, :])
                nc.tensor.matmul(ps[1][:, 0:2], wraw[:, 2 * D:3 * D], avec[:, :], start=True, stop=True)
                nc.tensor.matmul(ps[2][0:1, 0:2], bcol[:, :], avec[:, :], start=True,
                                 stop=True).then_inc(s_wt, 1)

            @block.vector
            def _(dve):
                link = Chain(dve, s_cdve)
                for g in range(2):
                    link(nc.vector.memset(G[g], 0.0))
                link(nc.vector.memset(colsum[:, :], 0.0))
                link(nc.vector.memset(ksum[:, :], 0.0))
                dve.wait_ge(s_const, 1)
                link(nc.vector.tensor_copy(ident16[:, :], ident[:, :]))
                for b in range(BITS):
                    link(nc.vector.tensor_scalar(fold[:, b, :], ident16[:, :], float(1 << (SHIFT + b)), None,
                                                 ALU.mult))
                dve.wait_ge(s_wt, 1)
                dve.wait_ge(s_w, 128)
                link(nc.vector.tensor_copy(wqkT[:, :], ps[0][:, 0:2 * D]))
                link(nc.vector.tensor_copy(wa[:, 0:D], ps[0][:, 2 * D:3 * D]))
                link(nc.vector.tensor_copy(wa[:, D:WA], ps[1][:, 0:2]))
                link(nc.vector.tensor_copy(ba[:, D:WA], ps[2][0:1, 0:2]))
                link(nc.vector.tensor_copy(ba[:, 0:D], brow[:, 0:D]))
                link(nc.vector.tensor_tensor(ba[:, D + 1:WA], ba[:, D + 1:WA], brow[:, D:D + 1], ALU.add))

        def spread(a, n):
            return a.unsqueeze(2).to_broadcast([P, a.shape[1], n])

        def table_stage(tag, second):
            s_var, s_std, s_h = sem(f"{tag}_variance"), sem(f"{tag}_deviation"), sem(f"{tag}_h")
            s_hT, s_hTc, s_pr = sem(f"{tag}_h_transposed"), sem(f"{tag}_hT_copied"), sem(f"{tag}_projected")
            s_sq, s_n2, s_nrm = sem(f"{tag}_squared"), sem(f"{tag}_norm2"), sem(f"{tag}_norm")
            s_rows, s_st, s_ch = sem(f"{tag}_rows"), sem(f"{tag}_stored"), sem(f"{tag}_dve_chain")
            stores = 1 if second else 4
            mean, var, dev, inv = st[:, 16:24], st[:, 0:8], st[:, 8:16], st[:, 24:32]
            norm2, norm = small[:, 0:16], small[:, 16:32]
            with nc.Block() as block:
                @block.sync
                def _(sp):
                    with sp.Fori(0, NB) as b:
                        sp.wait_ge(s_rows, b + 1)
                        if second:
                            sp.dma_start(hw_b[bass.ds(b, 1)].rearrange("o p s c -> (o p) s c"), tw).then_inc(s_st, 16)
                        else:
                            for tab, c, rows in ((qh_b, 0, qk[:, :, 0:D]), (qh_b, D, hb),
                                                 (kh_b, 0, qk[:, :, D:2 * D]), (kh_b, D, hb)):
                                sp.dma_start(tab[bass.ds(b, 1), :, :, c:c + D].rearrange("o p s c -> (o p) s c"),
                                             rows).then_inc(s_st, 16)
                    sp.wait_ge(s_st, 16 * stores * NB)

                @block.tensor
                def _(pe):
                    with pe.Fori(0, NB) as b:
                        pe.wait_ge(s_h, b + 1)
                        for s in range(TB):
                            last = nc.tensor.transpose(ps[s // 4][:, s % 4 * D:(s % 4 + 1) * D], hb[:, s, :],
                                                       ident[:, :])
                        last.then_inc(s_hT, 1)
                        pe.wait_ge(s_hTc, b + 1)
                        for s in range(TB):
                            o = ps[2 + s // 2][:, s % 2 * 256:s % 2 * 256 + (WA if second else 2 * D)]
                            if second:
                                nc.tensor.matmul(o, hT[:, s, :], wa[:, :], start=True, stop=False)
                                last = nc.tensor.matmul(o, ones[0:1, :], ba[:, :], start=False, stop=True)
                            else:
                                last = nc.tensor.matmul(o, hT[:, s, :], wqkT[:, :], start=True, stop=True)
                        last.then_inc(s_pr, 1)

                @block.scalar
                def _(act):
                    with act.Fori(0, NB) as b:
                        act.wait_ge(s_var, b + 1)
                        nc.scalar.activation(dev, var, ACT.Sqrt).then_inc(s_std, 1)
                        act.wait_ge(s_hT, b + 1)
                        for f in range(2):
                            last = nc.scalar.copy(hT[:, 4 * f:4 * f + 4, :],
                                                  ps[f][:, :].rearrange("p (s c) -> p s c", s=4))
                        last.then_inc(s_hTc, 1)
                        if not second:
                            act.wait_ge(s_pr, b + 1)
                            for f in range(4):
                                last = nc.scalar.activation(sq[:, 4 * f:4 * f + 4, :],
                                                            ps[2 + f][:, :].rearrange("p (s c) -> p s c", s=4),
                                                            ACT.Square)
                            last.then_inc(s_sq, 1)
                            act.wait_ge(s_n2, b + 1)
                            nc.scalar.activation(norm, norm2, ACT.Sqrt).then_inc(s_nrm, 1)

                @block.vector
                def _(dve):
                    link = Chain(dve, s_ch)

                    def batch(b, first):
                        xb = res[:, bass.ts(b, TB), :]
                        link(nc.vector.tensor_reduce(mean, xb, AX.X, ALU.add))
                        link(nc.vector.tensor_scalar(mean, mean, -1.0 / D, None, ALU.mult))
                        link(nc.vector.tensor_tensor(xc, xb, spread(mean, D), ALU.add))
                        link(nc.vector.tensor_tensor(sq[:, 0:TB, :], xc, xc, ALU.mult))
                        link(nc.vector.tensor_reduce(inv, sq[:, 0:TB, :], AX.X, ALU.add))
                        nc.vector.tensor_scalar(var, inv, 1.0 / D, EPS, ALU.mult, ALU.add).then_inc(s_var, 1)
                        dve.wait_ge(s_std, b + 1)
                        link(nc.vector.reciprocal(inv, dev))
                        if not first:
                            dve.wait_ge(s_st, 16 * stores * b)
                        nc.vector.scalar_tensor_tensor(out=hb, in0=xc, scalar=0.0, in1=spread(inv, D), op0=ALU.max,
                                                       op1=ALU.mult).then_inc(s_h, 1)
                        if second:
                            dve.wait_ge(s_pr, b + 1)
                            for f in range(4):
                                last = nc.vector.tensor_copy(
                                    tw[:, 2 * f:2 * f + 2, :],
                                    ps[2 + f][:, :].rearrange("p (s c) -> p s c", s=2)[:, :, 0:WA])
                            last.then_inc(s_rows, 1)
                            dve.wait_ge(s_rows, b + 1)
                            nc.vector.tensor_copy(s1_all[:, bass.ts(b, TB)], tw[:, :, D + 1])
                            link(nc.vector.tensor_reduce(meanb[:, :], tw[:, :, 0:D].rearrange("p s c -> p c s"),
                                                         AX.X, ALU.add))
                            link(nc.vector.tensor_tensor(colsum[:, :], colsum[:, :], meanb[:, :], ALU.add))
                        else:
                            dve.wait_ge(s_sq, b + 1)
                            nc.vector.tensor_reduce(norm2, sq, AX.X, ALU.add).then_inc(s_n2, 1)
                            dve.wait_ge(s_nrm, b + 1)
                            link(nc.vector.tensor_scalar(norm, norm, COS_EPS, None, ALU.max))
                            link(nc.vector.reciprocal(norm, norm))
                            for f in range(4):
                                last = nc.vector.tensor_tensor(
                                    qk[:, 2 * f:2 * f + 2, :].rearrange("p s (a c) -> p (s a) c", a=2),
                                    ps[2 + f][:, :].rearrange("p (s c) -> p s c", s=4),
                                    spread(norm[:, 4 * f:4 * f + 4], D), ALU.mult)
                            last.then_inc(s_rows, 1)

                    peel(dve, link, 0, NB, batch)

        table_stage("first", False)

        s_adj = [[sem(f"adj_loaded_{p}{f}") for f in "ab"] for p in range(2)]
        s_cast = [sem(f"adj_cast_{f}") for f in "ab"]
        s_key, s_keyu, s_mu = sem("keys_folded"), sem("keys_used"), [sem("m16a_used"), sem("m16b_used")]
        s_cnt, s_cntT, s_lists = sem("counts"), sem("counts_transposed"), sem("lists_ready")
        s_gate, s_pgate = sem("l0_dve_gate"), sem("l0_pool_gate")
        s_ch0, s_ipool = sem("l0_dve_chain"), sem("l0_pool_chain")
        s_g = [sem(f"l0_gathered_{p}") for p in range(2)]
        s_own = [sem(f"own_rows_{p}") for p in range(2)]
        s_sc, s_ex, s_dg, s_pv = sem("l0_scores"), sem("l0_exp"), sem("l0_diag"), sem("l0_weighted")
        s_res, s_pvu = sem("l0_rows_done"), sem("l0_pv_used")
        PAIRS = T // 2

        def gathers(pool, p, view, tab, s_got, k):
            for s in range(S):
                def one():
                    pool.indirect_dma_start(
                        out=view[:, s, :], out_offset=None, in_=tab,
                        in_offset=bass.IndirectOffsetOnAxis(ap=idx_st[p][:, s:s + 1], axis=0),
                        bounds_check=N - 1, oob_is_err=False).then_inc(s_got, 16)
                if s < S0:
                    one()
                else:
                    with pool.If(k > s):
                        one()
                    with pool.Else():
                        pool.nop()

        with nc.Block() as block:
            @block.sync
            def _(sp):
                def own_rows(i, first):
                    for p in range(2):
                        t = 2 * i + p
                        if not first:
                            sp.wait_ge(s_res, 2 * i + p - 1)
                        sp.dma_start(own[p], kh_t[bass.ds(t, 1)].rearrange("o p c -> (o p) c")).then_inc(s_own[p], 16)

                peel(sp, None, 0, PAIRS, own_rows)

            @block.gpsimd
            def _(pool):
                link = Chain(pool, s_ipool)

                def pair(i, first):
                    pool.wait_ge(s_lists, i + 1)
                    pool.sem_inc(s_pgate, 1)
                    for p in range(2):
                        t = 2 * i + p
                        k = pool.value_load(kmax_all[0:1, bass.ds(t, 1)], min_val=0, max_val=S)
                        if not first:
                            pool.wait_ge(s_pv, 2 * i + p - 1)
                            pool.sem_inc(s_pgate, 1)
                        link(nc.gpsimd.tensor_copy(idx_st[p][:, :], idx_all[:, bass.ts(t, S)]), s_pgate)
                        gathers(pool, p, G0[p], qh_tab, s_g[p], k)

                peel(pool, link, 0, PAIRS, pair)

            @block.scalar
            def _(act):
                def load(t, p, f):
                    lo, hi = ((0, CUT), (CUT, N))[f]
                    act.dma_start(adj_sb[p][f], adj_t[bass.ds(t, 1), :, lo:hi].rearrange(
                        "o p c -> (o p) c")).then_inc(s_adj[p][f], 16)

                def cast(i, first, more=True):
                    for p in range(2):
                        t = 2 * i + p
                        for f in range(2):
                            act.wait_ge(s_adj[p][f], 16 * (i + 1))
                            if not (first and p == 0):
                                act.wait_ge(s_mu[f], 2 * i + p)
                            nc.scalar.activation(m16[f], adj_sb[p][f], ACT.Copy,
                                                 accum_out=deg_all[:, bass.ds(2 * t + f, 1)]).then_inc(s_cast[f], 1)
                            if more:
                                act.wait_ge(s_cast[f], 2 * i + p + 1)
                                load(t + 2, p, f)

                def exps(i, first):
                    for p in range(2):
                        act.wait_ge(s_sc, 2 * i + p + 1)
                        nc.scalar.activation(prob[:, p, :], score[:, p, :], ACT.Exp).then_inc(s_ex, 1)

                for p in range(2):
                    for f in range(2):
                        load(p, p, f)
                cast(0, True)
                cast(1, False)

                def both(i, first):
                    cast(i, False)
                    exps(i - 2, first)
                peel(act, None, 2, PAIRS - 1, both)
                cast(PAIRS - 1, False, False)
                exps(PAIRS - 3, False)
                exps(PAIRS - 2, False)
                exps(PAIRS - 1, False)

            @block.tensor
            def _(pe):
                def folds(i, first):
                    for p in range(2):
                        if not first:
                            pe.wait_ge(s_keyu, 2 * i + p - 1)
                        for h in range(2):
                            o = ps[2 * p + h][:, 0:HW]
                            nc.tensor.matmul(o, ones16[:, :], w_hi[:, h * HW:(h + 1) * HW], start=True, stop=False)
                            nc.tensor.matmul(o, ones16[:, :], w_lo[:, h * HW:(h + 1) * HW], start=False, stop=False)
                        for f, bits in enumerate((range(0, BITS // 2), range(BITS // 2, BITS))):
                            pe.wait_ge(s_cast[f], 2 * i + p + 1)
                            for b in bits:
                                for h in range(2):
                                    n = HW if b < BITS - 1 or h == 0 else LAST - HW
                                    c = (b - f * (BITS // 2)) * WORDS + h * HW
                                    last = nc.tensor.matmul(ps[2 * p + h][:, 0:n], fold[:, b, :], m16[f][:, c:c + n],
                                                            start=False, stop=b == BITS - 1)
                            last.then_inc(s_mu[f], 1)
                        pe.wait_ge(s_mu[1], 2 * i + p + 1)
                        pe.sem_inc(s_key, 1)

                def counts(i):
                    pe.wait_ge(s_cnt, i + 1)
                    for p in range(2):
                        last = nc.tensor.matmul(ps[4][0:1, p * P:(p + 1) * P], cnt2[:, p:p + 1], ident[:, :],
                                                start=True, stop=True)
                    last.then_inc(s_cntT, 1)

                def weighted(i, first):
                    for p in range(2):
                        pe.wait_ge(s_dg, 2 * i + p + 1)
                        if not first:
                            pe.wait_ge(s_res, 2 * i + p - 1)
                        for s in range(S):
                            last = nc.tensor.matmul(ps[5 + p][:, 0:D], G0[p][:, s, 0:D], G0[p][:, s, D:2 * D],
                                                    start=s == 0, stop=s == S - 1)
                        last.then_inc(s_pv, 1)

                folds(0, True)
                counts(0)
                folds(1, False)

                def both(i, first):
                    counts(i - 1)
                    folds(i, False)
                    weighted(i - 2, first)
                peel(pe, None, 2, PAIRS, both)
                counts(PAIRS - 1)
                weighted(PAIRS - 2, False)
                weighted(PAIRS - 1, False)

            @block.vector
            def _(dve):
                link = Chain(dve, s_ch0)

                def lists(i, first):
                    for p in range(2):
                        dve.wait_ge(s_key, 2 * i + p + 1)
                        kp = [ps[2 * p + h] for h in range(2)]
                        for h in range(2):
                            last = nc.vector.tensor_copy(keys[:, h, :], kp[h][:, 0:HW])
                        last.then_inc(s_keyu, 1)
                        dve.wait_ge(s_keyu, 2 * i + p + 1)
                        dve.sem_inc(s_gate, 1)
                        for r in range(3):
                            link(nc.vector.max(top[:, p, 8 * r:8 * r + 8], keys[:, :, :]), s_gate)
                            if r < 2:
                                link(nc.vector.match_replace(keys[:, :, :], top[:, p, 8 * r:8 * r + 8],
                                                             keys[:, :, :], -1.0), s_gate)
                    link(nc.vector.tensor_copy(tbit[:, :, :], top[:, :, :]))
                    link(nc.vector.tensor_scalar(expo[:, :, :], tbit[:, :, :], (1 << SHIFT) - 1, None, ALU.bitwise_and))
                    link(nc.vector.tensor_tensor(left[:, :, :], top[:, :, :], expo[:, :, :], ALU.subtract))
                    link(nc.vector.tensor_scalar(wpos[:, :, :], expo[:, :, :], float(1 - EXP0 * WORDS), None, ALU.add))
                    for r in range(ROUNDS):
                        leftb = left[:, :, :].bitcast(i32)
                        link(nc.vector.tensor_scalar(expo[:, :, :], leftb, 23, None, ALU.logical_shift_right))
                        link(nc.vector.scalar_tensor_tensor(out=cand[:, :, r, :], in0=expo[:, :, :], scalar=float(WORDS),
                                                            in1=wpos[:, :, :], op0=ALU.mult, op1=ALU.add))
                        if r < ROUNDS - 1:
                            link(nc.vector.tensor_scalar(tbit[:, :, :], leftb, 0x7F800000, None, ALU.bitwise_and))
                            link(nc.vector.tensor_tensor(left[:, :, :], left[:, :, :],
                                                         tbit[:, :, :].bitcast(fp32), ALU.subtract))
                    dve.sem_inc(s_gate, 1)
                    for p in range(2):
                        c = cand[:, p, :, :]
                        for r in range(3):
                            link(nc.vector.max(nbr[:, p, 8 * r:8 * r + 8], c), s_gate)
                            if r < 2:
                                link(nc.vector.match_replace(c, nbr[:, p, 8 * r:8 * r + 8], c, -1e5), s_gate)
                    pair_idx = idx_all[:, bass.ts(i, 2 * S)]
                    flat = nbr[:, :, :].rearrange("p a s -> p (a s)")
                    none = keys[:, 0, 0:2 * S]
                    link(nc.vector.tensor_scalar(none, flat, 0.0, FAR_IDX, ALU.is_le, ALU.mult))
                    link(nc.vector.scalar_tensor_tensor(out=pair_idx, in0=flat, scalar=-1.0, in1=none, op0=ALU.add,
                                                        op1=ALU.add))
                    link(nc.vector.tensor_scalar(none, flat, 0.0, None, ALU.is_gt))
                    link(nc.vector.tensor_reduce(cnt2[:, :], keys[:, 0, 0:2 * S].rearrange("p (a s) -> p a s", a=2), AX.X, ALU.add))
                    nc.vector.tensor_copy(cnt_all[:, bass.ts(i, 2)], cnt2[:, :]).then_inc(s_cnt, 1)
                    dve.wait_ge(s_cntT, i + 1)
                    kmax = kmax_all[0:1, bass.ts(i, 2)]
                    link(nc.vector.tensor_reduce(kmax, ps[4][0:1, 0:2 * P].rearrange("o (a q) -> o a q", a=2), AX.X, ALU.max))
                    link(nc.vector.tensor_scalar(kput[:, :], kmax, float(S0), 16.0, ALU.max, ALU.mult))
                    link(nc.vector.tensor_tensor(ksum[:, :], ksum[:, :], kput[:, :], ALU.add))
                    nc.vector.tensor_copy(goal_all[0:1, bass.ts(i, 2)], ksum[:, :]).then_inc(s_lists, 1)

                def attend(i, first):
                    link(nc.vector.tensor_scalar(valid[:, :, :].rearrange("p a s -> p (a s)"), idx_all[:, bass.ts(i, 2 * S)], float(NONE), None, ALU.is_lt))
                    for p in range(2):
                        t = 2 * i + p
                        q = G0[p][:, :, 0:D]
                        goal = dve.value_load(goal_all[0:1, bass.ds(t, 1)], min_val=16 * S0, max_val=16 * S * T)
                        dve.wait_ge(s_g[p], goal)
                        dve.wait_ge(s_own[p], 16 * (i + 1))
                        link(nc.vector.tensor_tensor(q, q, own[p][:, 0:D].unsqueeze(1).to_broadcast([P, S, D]), ALU.mult))
                        nc.vector.tensor_reduce(score[:, p, :], q, AX.X, ALU.add).then_inc(s_sc, 1)
                        dve.wait_ge(s_ex, 2 * i + p + 1)
                        link(nc.vector.tensor_tensor(score[:, p, :], prob[:, p, :], valid[:, p, :], ALU.mult))
                        nc.vector.tensor_tensor(q, ident[:, :].unsqueeze(1).to_broadcast([P, S, D]),
                                                spread(score[:, p, :], D), ALU.mult).then_inc(s_dg, 1)
                        den, none, keep = st[:, p:p + 1], st[:, 2:3], st[:, 3:4]
                        link(nc.vector.tensor_reduce(den, score[:, p, :], AX.X, ALU.add))
                        link(nc.vector.tensor_scalar(none, cnt_all[:, bass.ds(t, 1)], 0.0, None, ALU.is_equal))
                        link(nc.vector.tensor_tensor(den, den, none, ALU.add))
                        link(nc.vector.reciprocal(den, den))
                        link(nc.vector.tensor_scalar(den, den, 1.0 - KEEP, None, ALU.mult))
                        link(nc.vector.tensor_scalar(keep, none, 1.0 - KEEP, KEEP, ALU.mult, ALU.add))
                        xr = row(t)
                        link(nc.vector.scalar_tensor_tensor(out=xr, in0=own[p][:, D:2 * D], scalar=keep, in1=xr,
                                                            op0=ALU.mult, op1=ALU.add))
                        if not (first and p == 0):
                            finish(t - 1, 1 - p)

                def row(t):
                    return res[:, bass.ds(t, 1), :].rearrange("p o c -> p (o c)")

                def finish(t, p):
                    dve.wait_ge(s_pv, t + 1)
                    nc.vector.scalar_tensor_tensor(out=row(t), in0=ps[5 + p][:, 0:D], scalar=st[:, p:p + 1],
                                                   in1=row(t), op0=ALU.mult, op1=ALU.add).then_inc(s_res, 1)

                lists(0, True)

                def both(i, first):
                    lists(i, False)
                    attend(i - 1, first)
                peel(dve, link, 1, PAIRS, both)
                attend(PAIRS - 1, False)
                finish(T - 1, 1)

        s_miss, s_missT, s_flag, s_chf = sem("missed"), sem("missed_transposed"), sem("flag_set"), sem("flag_chain")
        with nc.Block() as block:
            @block.vector
            def _(dve):
                link = Chain(dve, s_chf)
                link(nc.vector.tensor_reduce(s1_all[:, :], deg_all[:, :].rearrange("p (t f) -> p t f", f=2), AX.X,
                                             ALU.add))
                link(nc.vector.tensor_tensor(s1_all[:, :], s1_all[:, :], cnt_all[:, :], ALU.subtract))
                nc.vector.tensor_reduce(st[:, 0:1], s1_all[:, :], AX.X, ALU.max).then_inc(s_miss, 1)
                dve.wait_ge(s_missT, 1)
                nc.vector.tensor_reduce(flag[:, :], ps[0][0:1, 0:P], AX.X, ALU.max).then_inc(s_flag, 1)

            @block.tensor
            def _(pe):
                pe.wait_ge(s_miss, 1)
                nc.tensor.matmul(ps[0][0:1, 0:P], st[:, 0:1], ident[:, :], start=True, stop=True).then_inc(s_missT, 1)

        pos[0] = 0
        wide = take(N)
        adj_d = take(N).bitcast(i32)
        e_d = take(N)
        feat = take(T * D).rearrange("p (t c) -> p t c", t=T)
        own_d, kT, pT = take(2 * D), take(D), [take(512), take(512)]
        C = N // 512

        class Dense:

            def __init__(self, tag, second):
                self.second, self.tab, self.c0 = second, (hw_tab if second else qh_tab), (0 if second else D)
                self.x = sem(f"{tag}_x")
                self.feat = sem(f"{tag}_feat")
                self.row = sem(f"{tag}_row")
                self.wide_ps = sem(f"{tag}_wide_ps")
                self.wide = sem(f"{tag}_wide")
                self.adj = sem(f"{tag}_adj")
                self.own = sem(f"{tag}_own")
                self.k_ps = sem(f"{tag}_k_ps")
                self.kT = sem(f"{tag}_kT")
                self.scores = sem(f"{tag}_scores")
                self.exp = sem(f"{tag}_exp")
                self.masked = sem(f"{tag}_masked")
                self.blocks = sem(f"{tag}_blocks")
                self.blocks_sb = sem(f"{tag}_blocks_sb")
                self.summed = sem(f"{tag}_summed")
                self.rows = sem(f"{tag}_rows")
                self.stored = sem(f"{tag}_stored")
                self.chain = sem(f"{tag}_chain")

            def sync(self, sp):
                if not self.second:
                    x_t = x.rearrange("(t p) c -> p t c", p=P)
                    for b in range(NB):
                        sp.dma_start(res[:, b * TB:(b + 1) * TB, :], x_t[:, b * TB:(b + 1) * TB, :]).then_inc(self.x, 16)
                rows = self.tab.rearrange("(t p) c -> p t c", p=P)
                for b in range(NB):
                    sp.dma_start(feat[:, b * TB:(b + 1) * TB, :],
                                 rows[:, b * TB:(b + 1) * TB, self.c0:self.c0 + D]).then_inc(self.feat, 16)
                if self.second:
                    sp.dma_start(e_d[0:1, :], hw_tab[:, D:D + 1].rearrange("n o -> o n"),
                                 allow_slow_non_contiguous=True).then_inc(self.row, 16)
                else:
                    e_t = e_d.rearrange("p (t c) -> p t c", t=T)
                    for b in range(NB):
                        sp.dma_start(e_t[:, b * TB:(b + 1) * TB, :],
                                     rows[:, b * TB:(b + 1) * TB, 0:D]).then_inc(self.row, 16)

                def tile(t, first):
                    if not first:
                        sp.wait_ge(self.rows, t)
                    sp.dma_start(adj_d, adj_t[bass.ds(t, 1)].rearrange("o p c -> (o p) c")).then_inc(self.adj, 16)
                    if self.second:
                        sp.wait_ge(self.rows, t + 1)
                        sp.dma_start(out_t[bass.ds(t, 1)].rearrange("o p c -> (o p) c"), own_d[:, 0:D]).then_inc(self.stored, 16)
                    else:
                        sp.dma_start(own_d, kh_t[bass.ds(t, 1)].rearrange("o p c -> (o p) c")).then_inc(self.own, 16)
                peel(sp, None, 0, T, tile)
                if self.second:
                    sp.wait_ge(self.stored, 16 * T)

            def tensor(self, pe):
                pe.wait_ge(self.row, 16 if self.second else 16 * NB)
                for c in range(C):
                    if c >= 2:
                        pe.wait_ge(self.wide, c - 1)
                    if self.second:
                        last = nc.tensor.matmul(ps[c % 2][:, :], ones[0:1, :], e_d[0:1, c * 512:(c + 1) * 512],
                                                start=True, stop=True)
                    else:
                        for s in range(4):
                            a = c * 512 + s * P
                            last = nc.tensor.transpose(ps[c % 2][:, s * P:(s + 1) * P], e_d[:, a:a + P], ident[:, :])
                    last.then_inc(self.wide_ps, 1)
                pe.wait_ge(self.wide, C)
                pe.wait_ge(self.feat, 16 * NB)

                def tile(t, first):
                    if not self.second:
                        pe.wait_ge(self.own, 16 * (t + 1))
                        nc.tensor.transpose(ps[7][:, 0:P], own_d[:, 0:D], ident[:, :]).then_inc(self.k_ps, 1)
                        pe.wait_ge(self.kT, t + 1)
                        for c in range(C):
                            if not first or c >= 4:
                                pe.wait_ge(self.exp, C * t + c - 3)
                            nc.tensor.matmul(ps[c % 4][:, :], kT, wide[:, c * 512:(c + 1) * 512], start=True,
                                             stop=True).then_inc(self.scores, 1)
                    if not first:
                        pe.wait_ge(self.rows, t)

                    def add_up(c):
                        pe.wait_ge(self.blocks_sb, C * t + c + 1)
                        for s in range(4):
                            last = nc.tensor.matmul(ps[6][:, 0:D], pT[c % 2][:, s * P:(s + 1) * P],
                                                    feat[:, 4 * c + s, :], start=c == 0 and s == 0,
                                                    stop=c == C - 1 and s == 3)
                        last.then_inc(self.summed, 1)

                    for c in range(C):
                        pe.wait_ge(self.masked, t + 1 if self.second else C * t + c + 1)
                        for s in range(4):
                            a = c * 512 + s * P
                            last = nc.tensor.transpose(ps[4 + c % 2][:, s * P:(s + 1) * P], e_d[:, a:a + P], ident[:, :])
                        last.then_inc(self.blocks, 1)
                        if c >= 1:
                            add_up(c - 1)
                    add_up(C - 1)
                peel(pe, None, 0, T, tile)

            def scalar(self, act):
                def tile(t, first):
                    if self.second:
                        act.wait_ge(self.scores, t + 1)
                        nc.scalar.activation(e_d, e_d, ACT.Exp, bias=st[:, 1:2], accum_out=st[:, 4:5]).then_inc(self.masked, 1)
                    else:
                        for c in range(C):
                            act.wait_ge(self.scores, C * t + c + 1)
                            if not first:
                                act.wait_ge(self.rows, t)
                            nc.scalar.activation(e_d[:, c * 512:(c + 1) * 512], ps[c % 4][:, :],
                                                 ACT.Exp).then_inc(self.exp, 1)
                    for c in range(C):
                        act.wait_ge(self.blocks, C * t + c + 1)
                        if not first or c >= 2:
                            act.wait_ge(self.summed, C * t + c - 1)
                        nc.scalar.copy(pT[c % 2], ps[4 + c % 2][:, :]).then_inc(self.blocks_sb, 1)
                peel(act, None, 0, T, tile)

            def vector(self, dve):
                link = Chain(dve, self.chain)
                for c in range(C):
                    dve.wait_ge(self.wide_ps, c + 1)
                    nc.vector.tensor_copy(wide[:, c * 512:(c + 1) * 512], ps[c % 2][:, :]).then_inc(self.wide, 1)
                if not self.second:
                    dve.wait_ge(self.x, 16 * NB)
                dve.wait_ge(self.wide, C)
                top_s, far, den, none, keep = (st[:, c:c + 1] for c in (0, 1, 4, 5, 6))

                def row(t):
                    return res[:, bass.ds(t, 1), :].rearrange("p o c -> p (o c)")

                def first_layer(t, first):
                    dve.wait_ge(self.k_ps, t + 1)
                    nc.vector.tensor_copy(kT, ps[7][:, 0:P]).then_inc(self.kT, 1)
                    dve.wait_ge(self.adj, 16 * (t + 1))
                    for c in range(C):
                        cols = slice(c * 512, (c + 1) * 512)
                        dve.wait_ge(self.exp, C * t + c + 1)
                        nc.vector.tensor_tensor(e_d[:, cols], e_d[:, cols], adj_d[:, cols], ALU.mult).then_inc(self.masked, 1)
                    dve.wait_ge(self.masked, C * t + C)
                    link(nc.vector.tensor_reduce(den, e_d, AX.X, ALU.add))
                    link(nc.vector.tensor_scalar(none, den, 0.0, None, ALU.is_equal))
                    link(nc.vector.tensor_tensor(den, den, none, ALU.add))
                    link(nc.vector.reciprocal(den, den))
                    link(nc.vector.tensor_scalar(den, den, 1.0 - KEEP, None, ALU.mult))
                    link(nc.vector.tensor_scalar(keep, none, 1.0 - KEEP, KEEP, ALU.mult, ALU.add))
                    link(nc.vector.scalar_tensor_tensor(out=row(t), in0=own_d[:, D:2 * D], scalar=keep, in1=row(t),
                                                        op0=ALU.mult, op1=ALU.add))
                    dve.wait_ge(self.summed, C * t + C)
                    nc.vector.scalar_tensor_tensor(out=row(t), in0=ps[6][:, 0:D], scalar=den, in1=row(t),
                                                   op0=ALU.mult, op1=ALU.add).then_inc(self.rows, 1)

                def second_layer(t, first):
                    s1 = s1_all[:, bass.ds(t, 1)]
                    dve.wait_ge(self.adj, 16 * (t + 1))
                    link(nc.vector.tensor_scalar(e_d, adj_d, -1.0, FAR, ALU.add, ALU.mult))
                    link(nc.vector.tensor_tensor(e_d, e_d, wide, ALU.add))
                    link(nc.vector.tensor_scalar(e_d, e_d, s1, None, ALU.add))
                    link(nc.vector.scalar_tensor_tensor(out=e_d, in0=e_d, scalar=LEAK, in1=e_d, op0=ALU.mult, op1=ALU.max))
                    link(nc.vector.tensor_reduce(top_s, e_d, AX.X, ALU.max))
                    nc.vector.tensor_scalar(far, top_s, -1.0, None, ALU.mult).then_inc(self.scores, 1)
                    dve.wait_ge(self.masked, t + 1)
                    link(nc.vector.reciprocal(den, den))
                    if not first:
                        dve.wait_ge(self.stored, 16 * t)
                    dve.wait_ge(self.summed, C * t + C)
                    nc.vector.scalar_tensor_tensor(out=own_d[:, 0:D], in0=ps[6][:, 0:D], scalar=den, in1=row(t),
                                                   op0=ALU.mult, op1=ALU.add).then_inc(self.rows, 1)
                peel(dve, link, 0, T, second_layer if self.second else first_layer)

        def load_flag(eng):
            return eng.value_load(flag[0:1, 0:1], min_val=0, max_val=N)

        dense0 = Dense("dense0", False)
        with nc.Block() as block:
            def redo(eng, part):
                with eng.If(load_flag(eng) > 0):
                    part(eng)
                with eng.Else():
                    eng.nop()

            @block.sync
            def _(sp):
                redo(sp, dense0.sync)

            @block.tensor
            def _(pe):
                redo(pe, dense0.tensor)

            @block.scalar
            def _(act):
                redo(act, dense0.scalar)

            @block.vector
            def _(dve):
                redo(dve, dense0.vector)

        table_stage("second", True)

        s_cs, s_mean = sem("column_sums"), sem("mean_row")
        s_g1 = [sem(f"l1_gathered_{p}") for p in range(2)]
        s_sc1, s_ex1, s_dg1, s_pv1 = sem("l1_scores"), sem("l1_exp"), sem("l1_diag"), sem("l1_weighted")
        s_rows1, s_out1 = sem("l1_rows"), [sem(f"l1_stored_{p}") for p in range(2)]
        s_ch1, s_pch1, s_pgate1 = sem("l1_dve_chain"), sem("l1_pool_chain"), sem("l1_pool_gate")
        dense1 = Dense("dense1", True)

        def lists_sync(sp):
            def pair(i, first):
                for p in range(2):
                    sp.wait_ge(s_rows1, 2 * i + p + 1)
                    sp.dma_start(out_t[bass.ds(2 * i + p, 1)].rearrange("o p c -> (o p) c"),
                                 outb[p]).then_inc(s_out1[p], 16)
            peel(sp, None, 0, PAIRS, pair)
            for p in range(2):
                sp.wait_ge(s_out1[p], 16 * PAIRS)

        def lists_gpsimd(pool):
            link = Chain(pool, s_pch1)

            def pair(i, first):
                for p in range(2):
                    t = 2 * i + p
                    k = pool.value_load(kmax_all[0:1, bass.ds(t, 1)], min_val=0, max_val=S)
                    if not first:
                        pool.wait_ge(s_pv1, 2 * i + p - 1)
                        pool.sem_inc(s_pgate1, 1)
                    link(nc.gpsimd.tensor_copy(idx_st[p][:, :], idx_all[:, bass.ts(t, S)]), s_pgate1)
                    gathers(pool, p, G1[p], hw_tab, s_g1[p], k)
            peel(pool, link, 0, PAIRS, pair)

        def lists_scalar(act):
            def pair(i, first):
                for p in range(2):
                    act.wait_ge(s_sc1, 2 * i + p + 1)
                    nc.scalar.activation(prob[:, p, :], score[:, p, :], ACT.Exp, bias=st[:, 4 + p:5 + p],
                                         accum_out=st[:, 6 + p:7 + p]).then_inc(s_ex1, 1)
            peel(act, None, 0, PAIRS, pair)

        def lists_tensor(pe):
            pe.wait_ge(s_cs, 1)
            nc.tensor.matmul(ps[7][:, 0:D], ones[:, :], colsum[:, :], start=True, stop=True).then_inc(s_mean, 1)

            def pair(i, first):
                for p in range(2):
                    pe.wait_ge(s_dg1, 2 * i + p + 1)
                    if not first:
                        pe.wait_ge(s_rows1, 2 * i + p - 1)
                    for s in range(S):
                        last = nc.tensor.matmul(ps[5 + p][:, 0:D], diag1[p][:, s, :], G1[p][:, s, 0:D],
                                                start=s == 0, stop=s == S - 1)
                    last.then_inc(s_pv1, 1)
            peel(pe, None, 0, PAIRS, pair)

        def lists_vector(dve):
            link = Chain(dve, s_ch1)
            dve.sem_inc(s_cs, 1)
            dve.wait_ge(s_mean, 1)
            link(nc.vector.tensor_scalar(meanb[:, :], ps[7][:, 0:D], 1.0 / N, None, ALU.mult))

            def finish(t, p):
                dve.wait_ge(s_pv1, t + 1)
                nc.vector.scalar_tensor_tensor(out=outb[p], in0=ps[5 + p][:, 0:D], scalar=st[:, 6 + p:7 + p],
                                               in1=outb[p], op0=ALU.mult, op1=ALU.add).then_inc(s_rows1, 1)

            def pair(i, first):
                link(nc.vector.tensor_scalar(valid[:, :, :].rearrange("p a s -> p (a s)"),
                                             idx_all[:, bass.ts(i, 2 * S)], float(NONE), None, ALU.is_lt))
                link(nc.vector.tensor_scalar(negm[:, :, :], valid[:, :, :], -1.0, FAR, ALU.add, ALU.mult))
                for p in range(2):
                    t = 2 * i + p
                    sc, pr, none = score[:, p, :], prob[:, p, :], st[:, 2:3]
                    less, den = st[:, 4 + p:5 + p], st[:, 6 + p:7 + p]
                    goal = dve.value_load(goal_all[0:1, bass.ds(t, 1)], min_val=16 * S0, max_val=16 * S * T)
                    dve.wait_ge(s_g1[p], goal)
                    link(nc.vector.tensor_scalar(sc, G1[p][:, :, D], s1_all[:, bass.ds(t, 1)], None, ALU.add))
                    link(nc.vector.scalar_tensor_tensor(out=sc, in0=sc, scalar=LEAK, in1=sc, op0=ALU.mult, op1=ALU.max))
                    link(nc.vector.tensor_tensor(sc, sc, valid[:, p, :], ALU.mult))
                    link(nc.vector.tensor_tensor(sc, sc, negm[:, p, :], ALU.add))
                    link(nc.vector.tensor_reduce(less, sc, AX.X, ALU.max))
                    nc.vector.tensor_scalar(less, less, -1.0, None, ALU.mult).then_inc(s_sc1, 1)
                    dve.wait_ge(s_ex1, 2 * i + p + 1)
                    nc.vector.tensor_tensor(diag1[p], ident[:, :].unsqueeze(1).to_broadcast([P, S, D]), spread(pr, D),
                                            ALU.mult).then_inc(s_dg1, 1)
                    link(nc.vector.tensor_scalar(none, cnt_all[:, bass.ds(t, 1)], 0.0, None, ALU.is_equal))
                    link(nc.vector.reciprocal(den, den))
                    link(nc.vector.tensor_scalar(st[:, 3:4], none, -1.0, 1.0, ALU.mult, ALU.add))
                    link(nc.vector.tensor_tensor(den, den, st[:, 3:4], ALU.mult))
                    if not first:
                        dve.wait_ge(s_out1[p], 16 * i)
                    link(nc.vector.scalar_tensor_tensor(out=outb[p], in0=meanb[:, :], scalar=none,
                                                        in1=res[:, bass.ds(t, 1), :].rearrange("p o c -> p (o c)"),
                                                        op0=ALU.mult, op1=ALU.add))
                    if not (first and p == 0):
                        finish(t - 1, 1 - p)
            peel(dve, link, 0, PAIRS, pair)
            finish(T - 1, 1)

        with nc.Block() as block:
            def either(eng, dense, lists):
                with eng.If(load_flag(eng) > 0):
                    dense(eng)
                    eng.nop()
                with eng.Else():
                    lists(eng)
                    eng.nop()

            @block.sync
            def _(sp):
                either(sp, dense1.sync, lists_sync)

            @block.gpsimd
            def _(pool):
                either(pool, lambda e: None, lists_gpsimd)

            @block.tensor
            def _(pe):
                either(pe, dense1.tensor, lists_tensor)

            @block.scalar
            def _(act):
                either(act, dense1.scalar, lists_scalar)

            @block.vector
            def _(dve):
                either(dve, dense1.vector, lists_vector)


_INS = ['x', 'adj', 'L0_gnn_Wq', 'L0_gnn_Wk', 'L1_gnn_W', 'L1_gnn_b_W', 'L1_gnn_a_vec', 'L1_gnn_b_a']
_OUTS = [((8192, 128), 'float32')]


def kernel(**inputs):
    import numpy as _np
    import concourse.bacc as _bacc
    from concourse import mybir as _mybir
    from concourse.bass_utils import run_bass_kernel_spmd as _run

    nc = _bacc.Bacc("TRN2", target_bir_lowering=False, num_devices=1)
    arrays, args = {}, []
    for name in _INS:
        a = _np.ascontiguousarray(inputs[name])
        arrays[f"in_{name}_dram"] = a
        args.append(nc.dram_tensor(f"in_{name}_dram", a.shape, _mybir.dt.from_np(a.dtype), kind="ExternalInput").ap())
    for i, (shape, dtype) in enumerate(_OUTS):
        dt = _mybir.dt.from_np(_np.dtype(dtype))
        args.append(nc.dram_tensor(f"out_{i}_dram", shape, dt, kind="ExternalOutput").ap())
    adjacency_layers(nc, *args)
    r = _run(nc, [arrays], core_ids=[0])
    return r.results[0]["out_0_dram"]
```

```python
import concourse.bass as bass
from concourse import mybir
from contextlib import ExitStack


class Chain:

    def __init__(self, eng, sem):
        self.eng, self.sem, self.at, self.n = eng, sem, 0, 0

    def __call__(self, instruction, gate=None):
        self.n += 1
        instruction.then_inc(self.sem, 1)
        self.eng.wait_ge(self.sem, self.at + self.n)
        if gate is not None:
            self.eng.sem_inc(gate, 1)

    def add(self, instruction):
        self.n += 1
        instruction.then_inc(self.sem, 1)
        return self.n

    def wait(self, n, gate=None):
        self.eng.wait_ge(self.sem, self.at + n)
        if gate is not None:
            self.eng.sem_inc(gate, 1)

    def loop(self, i, first, per):
        self.start, self.first, self.per = self.at + self.n, first, per
        self.at, self.n = self.start + (i - first) * per, 0

    def ended(self, end):
        assert self.n == self.per, (self.n, self.per)
        self.at, self.n = self.start + (end - self.first) * self.per, 0


def peel(eng, link, first, end, body):
    before = link.n if link else 0
    body(first, True)
    per = link.n - before if link else 0
    with eng.Fori(first + 1, end) as i:
        if link:
            link.loop(i, first + 1, per)
        body(i, False)
    if link:
        link.ended(end)


def adjacency_layers(nc, x, adj, wq, wk, w, b_w, a_vec, b_a, out):
    fp32, bf16, i32 = mybir.dt.float32, mybir.dt.bfloat16, mybir.dt.int32
    ALU, ACT, AX = mybir.AluOpType, mybir.ActivationFunctionType, mybir.AxisListType

    N, D = x.shape
    P = 128
    T = N // P
    TB = 8
    NB = T // TB
    S = 24
    S0 = 8
    SIZES = [12, 16, S]
    ACT_DIAG = 8
    ROUNDS = 3
    BITS, SHIFT = 14, 10
    WORDS = -(-N // BITS)
    HW = WORDS // 2
    LAST = N - (BITS - 1) * WORDS
    CUT = BITS // 2 * WORDS
    assert WORDS % 2 == 0 and WORDS <= 1 << SHIFT and BITS + SHIFT <= 24
    EXP0 = 127 + SHIFT
    NONE = 8192
    assert N == NONE
    FAR_IDX = float(1 << 20)
    EPS, COS_EPS, LEAK, KEEP = 1e-5, 1e-4, 0.2, 0.5
    FAR = 3e38
    WA = D + 2

    qh_tab = nc.dram_tensor("qh_tab", (N, 2 * D), fp32).ap()
    kh_tab = nc.dram_tensor("kh_tab", (N, 2 * D), fp32).ap()
    hw_tab = nc.dram_tensor("hw_tab", (N, WA), fp32).ap()
    qh_b = qh_tab.rearrange("(b s p) c -> b p s c", p=P, s=TB)
    kh_b = kh_tab.rearrange("(b s p) c -> b p s c", p=P, s=TB)
    hw_b = hw_tab.rearrange("(b s p) c -> b p s c", p=P, s=TB)
    qh_t = qh_tab.rearrange("(t p) c -> t p c", p=P)
    kh_t = kh_tab.rearrange("(t p) c -> t p c", p=P)
    hw_t = hw_tab.rearrange("(t p) c -> t p c", p=P)
    adj_t = adj.rearrange("(t p) c -> t p c", p=P)
    out_t = out.rearrange("(t p) c -> t p c", p=P)

    ctx = ExitStack()
    with ctx:
        def sb(name, shape, dt=fp32):
            return ctx.enter_context(nc.sbuf_tensor(name, shape, dt))

        def sem(name):
            return ctx.enter_context(nc.semaphore(name))

        ident = sb("ident", [P, P])
        ident16 = sb("ident16", [P, P], bf16)
        ones = sb("ones", [P, P])
        ones16 = sb("ones16", [1, P], bf16)
        fold = sb("fold", [P, BITS, P], bf16)
        w_hi = sb("w_hi", [1, 19 * 32], bf16)
        w_lo = sb("w_lo", [1, 19 * 32], bf16)
        wqkT = sb("wqkT", [P, 2 * D])
        wa = sb("wa", [P, WA])
        ba = sb("ba", [1, WA])
        wraw = sb("wraw", [P, 3 * D])
        avec = sb("avec", [P, 2])
        bcol = sb("bcol", [P, 1])
        brow = sb("brow", [1, D + 1])
        res = sb("res", [P, T, D])
        idx_all = sb("idx_all", [P, T * S], i32)
        cnt_all = sb("cnt_all", [P, T])
        deg_all = sb("deg_all", [P, 2 * T])
        kmax_all = sb("kmax_all", [1, T], i32)
        goal_all = sb("goal_all", [1, T], i32)
        kput = sb("kput", [1, 2])
        ksum = sb("ksum", [1, 2])
        s1_all = sb("s1_all", [P, T])
        colsum = sb("colsum", [P, D])
        meanb = sb("meanb", [P, D])
        flag = sb("flag", [1, 1], i32)
        small = sb("small", [P, 64])

        G_W = S * (WA + D)
        assert G_W >= S * 2 * D

        arena = sb("arena", [P, 2 * N + N // 2 + 16 + 2 * G_W + 12 * D])

        pos = [0]

        def take(n):
            n += n % 2
            pos[0] += n
            return arena[:, pos[0] - n:pos[0]]

        def rows_of(n, width=D):
            return take(n * width).rearrange("p (s c) -> p s c", s=n)
        xc, xsq, qksq = rows_of(TB), rows_of(TB), rows_of(2 * TB)
        hb, hh, hT = ([rows_of(TB) for _ in range(2)] for _ in range(3))
        qk = [rows_of(TB, 2 * D) for _ in range(2)]
        tw = [rows_of(TB, WA) for _ in range(2)]
        pos[0] = 0
        adj_sb = [[take(CUT).bitcast(i32), take(N - CUT).bitcast(i32)] for _ in range(2)]
        m16 = [take(CUT // 2).bitcast(bf16)[:, 0:CUT], take((N - CUT) // 2).bitcast(bf16)[:, 0:N - CUT]]
        G = [take(G_W) for _ in range(2)]
        own = [take(2 * D) for _ in range(2)]
        outb = [take(D) for _ in range(2)]
        G0 = [g[:, 0:S * 2 * D].rearrange("p (s c) -> p s c", s=S) for g in G]
        G1 = [g[:, 0:S * WA].rearrange("p (s c) -> p s c", s=S) for g in G]
        diag1 = [g[:, S * WA:S * (WA + D)].rearrange("p (s c) -> p s c", s=S) for g in G]
        idx_st = [sb(f"idx_st{p}", [P, S], i32) for p in range(2)]
        top = sb("top", [P, 2, S])
        keys = sb("keys", [P, 2, 2, HW])
        wpos = sb("wpos", [P, 2, S])
        left = [sb(f"left{r}", [P, 2, S])[:, :, :] for r in range(ROUNDS)]
        got, none_at = sb("got", [P, 2 * S]), sb("none_at", [P, 2 * S])
        keyi, wi = sb("keyi", [P, 2, S], i32), sb("wi", [P, 2, S], i32)
        tbit = [sb(f"tbit{r}", [P, 2, S], i32) for r in range(ROUNDS)]
        expo = [sb(f"expo{r}", [P, 2, S], i32) for r in range(ROUNDS)]
        cnt2 = sb("cnt2", [P, 2])
        cand = sb("cand", [P, 2, ROUNDS, S])
        nbr = sb("nbr", [P, 2, S])
        valid = sb("valid", [P, 2, S])
        score = sb("score", [P, 2, S])
        weight = sb("weight", [P, 2, S + 1])
        own_diag = [sb(f"own_diag{p}", [P, D]) for p in range(2)]
        prob = sb("prob", [P, 2, S])
        negm = sb("negm", [P, 2, S])
        st = sb("st", [P, 32])

        key_ps = ctx.enter_context(nc.psum_tensor("key_ps", [P, 4, 512], fp32))
        ps = [key_ps[:, i, :] for i in range(4)]
        ps += [ctx.enter_context(nc.psum_tensor(f"ps{i}", [P, 512], fp32))[:, :] for i in range(4, 8)]

        s_w, s_x, s_const = sem("weights_loaded"), sem("x_loaded"), sem("constants_made")
        s_wt, s_cpool, s_cdve = sem("weights_transposed"), sem("const_pool_chain"), sem("const_dve_chain")
        with nc.Block() as block:
            @block.sync
            def _(sp):
                sp.dma_start(wraw[:, 0:D], wq).then_inc(s_w, 16)
                sp.dma_start(wraw[:, D:2 * D], wk).then_inc(s_w, 16)
                sp.dma_start(wraw[:, 2 * D:3 * D], w).then_inc(s_w, 16)
                sp.dma_start(avec[:, 0:1], a_vec[D:2 * D].rearrange("(p o) -> p o", o=1)).then_inc(s_w, 16)
                sp.dma_start(avec[:, 1:2], a_vec[0:D].rearrange("(p o) -> p o", o=1)).then_inc(s_w, 16)
                sp.dma_start(bcol[:, :], b_w.rearrange("(p o) -> p o", o=1)).then_inc(s_w, 16)
                sp.dma_start(brow[:, 0:D], b_w.rearrange("(o p) -> o p", o=1)).then_inc(s_w, 16)
                sp.dma_start(brow[:, D:D + 1], b_a.rearrange("(o p) -> o p", o=1)).then_inc(s_w, 16)
                x_t = x.rearrange("(t p) c -> p t c", p=P)
                for b in range(NB):
                    sp.dma_start(res[:, b * TB:(b + 1) * TB, :], x_t[:, b * TB:(b + 1) * TB, :]).then_inc(s_x, 16)
                sp.wait_ge(s_x, 16 * NB)

            @block.gpsimd
            def _(pool):
                link = Chain(pool, s_cpool)
                link(nc.gpsimd.memset(ident[:, :], 0.0))
                link(nc.gpsimd.affine_select(out=ident[:, :], in_=ident[:, :], compare_op=ALU.not_equal,
                                             fill=1.0, base=0, pattern=[[-1, P]], channel_multiplier=1))
                link(nc.gpsimd.memset(ones[:, :], 1.0))
                link(nc.gpsimd.memset(ones16[:, :], 1.0))
                link(nc.gpsimd.iota(w_hi[:, :], [[32, 19], [0, 32]], base=0, channel_multiplier=0,
                                    allow_small_or_imprecise_dtypes=True))
                nc.gpsimd.iota(w_lo[:, :], [[0, 19], [1, 32]], base=0, channel_multiplier=0,
                               allow_small_or_imprecise_dtypes=True).then_inc(s_const, 1)

            @block.tensor
            def _(pe):
                pe.wait_ge(s_w, 128)
                pe.wait_ge(s_const, 1)
                for k in range(3):
                    nc.tensor.transpose(ps[0][:, k * D:(k + 1) * D], wraw[:, k * D:(k + 1) * D], ident[:, :])
                nc.tensor.matmul(ps[1][:, 0:2], wraw[:, 2 * D:3 * D], avec[:, :], start=True, stop=True)
                nc.tensor.matmul(ps[2][0:1, 0:2], bcol[:, :], avec[:, :], start=True,
                                 stop=True).then_inc(s_wt, 1)

            @block.vector
            def _(dve):
                link = Chain(dve, s_cdve)
                for g in range(2):
                    link(nc.vector.memset(G[g], 0.0))
                link(nc.vector.memset(colsum[:, :], 0.0))
                link(nc.vector.memset(ksum[:, :], 0.0))
                dve.wait_ge(s_const, 1)
                link(nc.vector.tensor_copy(ident16[:, :], ident[:, :]))
                for b in range(BITS):
                    link(nc.vector.tensor_scalar(fold[:, b, :], ident16[:, :], float(1 << (SHIFT + b)), None,
                                                 ALU.mult))
                dve.wait_ge(s_wt, 1)
                dve.wait_ge(s_w, 128)
                link(nc.vector.tensor_copy(wqkT[:, :], ps[0][:, 0:2 * D]))
                link(nc.vector.tensor_copy(wa[:, 0:D], ps[0][:, 2 * D:3 * D]))
                link(nc.vector.tensor_copy(wa[:, D:WA], ps[1][:, 0:2]))
                link(nc.vector.tensor_copy(ba[:, D:WA], ps[2][0:1, 0:2]))
                link(nc.vector.tensor_copy(ba[:, 0:D], brow[:, 0:D]))
                link(nc.vector.tensor_tensor(ba[:, D + 1:WA], ba[:, D + 1:WA], brow[:, D:D + 1], ALU.add))

        def spread(a, n):
            return a.unsqueeze(2).to_broadcast([P, a.shape[1], n])

        def table_stage(tag, second):
            s_var, s_std, s_h = sem(f"{tag}_variance"), sem(f"{tag}_deviation"), sem(f"{tag}_h")
            s_hT, s_hTc, s_pr = sem(f"{tag}_h_transposed"), sem(f"{tag}_hT_copied"), sem(f"{tag}_projected")
            s_sq, s_n2, s_nrm = sem(f"{tag}_squared"), sem(f"{tag}_norm2"), sem(f"{tag}_norm")
            s_rows, s_ch = sem(f"{tag}_rows"), sem(f"{tag}_dve_chain")
            s_st = [sem(f"{tag}_stored_{p}") for p in range(2)]
            stores = 1 if second else 4
            mean, inv, var, dev = (st[:, c:c + TB] for c in (0, 8, 16, 24))
            norm2, norm = small[:, 0:16], small[:, 16:32]

            def steps(eng, link, step):
                def two(j, first):
                    for p in range(2):
                        step(2 * j + p, j, p, first, True)
                peel(eng, link, 0, NB // 2 - 1, two)
                step(NB - 2, NB // 2 - 1, 0, False, True)
                step(NB - 1, NB // 2 - 1, 1, False, False)

            with nc.Block() as block:
                @block.sync
                def _(sp):
                    with sp.Fori(0, NB // 2) as j:
                        for p in range(2):
                            b = 2 * j + p
                            sp.wait_ge(s_rows, b + 1)
                            if second:
                                sp.dma_start(hw_b[bass.ds(b, 1)].rearrange("o p s c -> (o p) s c"),
                                             tw[p]).then_inc(s_st[p], 16)
                                continue
                            for tab, c, rows in ((qh_b, 0, qk[p][:, :, 0:D]), (qh_b, D, hh[p]),
                                                 (kh_b, 0, qk[p][:, :, D:2 * D]), (kh_b, D, hh[p])):
                                sp.dma_start(tab[bass.ds(b, 1), :, :, c:c + D].rearrange("o p s c -> (o p) s c"),
                                             rows).then_inc(s_st[p], 16)
                    for p in range(2):
                        sp.wait_ge(s_st[p], 16 * stores * (NB // 2))

                @block.tensor
                def _(pe):
                    def transposes(b, p):
                        pe.wait_ge(s_h, b + 1)
                        for s in range(TB):
                            last = nc.tensor.transpose(ps[s // 4][:, s % 4 * D:(s % 4 + 1) * D], hb[p][:, s, :],
                                                       ident[:, :])
                        last.then_inc(s_hT, 1)

                    def step(b, j, p, first, more):
                        pe.wait_ge(s_hTc, b + 1)
                        if not (first and p == 0):
                            pe.wait_ge(s_rows, b)
                        for s in range(TB):
                            o = ps[4 + s // 2][:, s % 2 * 256:s % 2 * 256 + (WA if second else 2 * D)]
                            if second:
                                nc.tensor.matmul(o, hT[p][:, s, :], wa[:, :], start=True, stop=False)
                                last = nc.tensor.matmul(o, ones[0:1, :], ba[:, :], start=False, stop=True)
                            else:
                                last = nc.tensor.matmul(o, hT[p][:, s, :], wqkT[:, :], start=True, stop=True)
                        last.then_inc(s_pr, 1)
                        if more:
                            transposes(b + 1, 1 - p)

                    transposes(0, 0)
                    steps(pe, None, step)

                @block.scalar
                def _(act):
                    def root(b):
                        act.wait_ge(s_var, b + 1)
                        nc.scalar.activation(dev, var, ACT.Sqrt).then_inc(s_std, 1)

                    def copies(b, p):
                        act.wait_ge(s_hT, b + 1)
                        for f in range(2):
                            last = nc.scalar.copy(hT[p][:, 4 * f:4 * f + 4, :],
                                                  ps[f][:, :].rearrange("p (s c) -> p s c", s=4))
                        last.then_inc(s_hTc, 1)

                    def step(b, j, p, first, more):
                        if not second:
                            act.wait_ge(s_pr, b + 1)
                            for f in range(4):
                                last = nc.scalar.activation(qksq[:, 4 * f:4 * f + 4, :],
                                                            ps[4 + f][:, :].rearrange("p (s c) -> p s c", s=4),
                                                            ACT.Square)
                            last.then_inc(s_sq, 1)
                        if more:
                            root(b + 1)
                        if not second:
                            act.wait_ge(s_n2, b + 1)
                            nc.scalar.activation(norm, norm2, ACT.Sqrt).then_inc(s_nrm, 1)
                        if more:
                            copies(b + 1, 1 - p)

                    root(0)
                    copies(0, 0)
                    steps(act, None, step)

                @block.vector
                def _(dve):
                    link = Chain(dve, s_ch)

                    def variance(b):
                        xb = res[:, bass.ts(b, TB), :]
                        link(nc.vector.tensor_reduce(mean, xb, AX.X, ALU.add))
                        link(nc.vector.tensor_scalar(mean, mean, -1.0 / D, None, ALU.mult))
                        link(nc.vector.tensor_tensor(xc, xb, spread(mean, D), ALU.add))
                        link(nc.vector.tensor_tensor(xsq, xc, xc, ALU.mult))
                        link(nc.vector.tensor_reduce(inv, xsq, AX.X, ALU.add))
                        nc.vector.tensor_scalar(var, inv, 1.0 / D, EPS, ALU.mult, ALU.add).then_inc(s_var, 1)

                    def normalise(b, j, p, first):
                        dve.wait_ge(s_std, b + 1)
                        link(nc.vector.reciprocal(inv, dev))
                        nc.vector.scalar_tensor_tensor(out=hb[p], in0=xc, scalar=0.0, in1=spread(inv, D), op0=ALU.max,
                                                       op1=ALU.mult).then_inc(s_h, 1)
                        if not second:
                            xb = res[:, bass.ts(b, TB), :]
                            dve.wait_ge(s_h, b + 1)
                            if not first:
                                dve.wait_ge(s_st[p], 16 * stores * j)
                            link(nc.vector.tensor_scalar(hh[p], hb[p], 1.0 - KEEP, None, ALU.mult))
                            link(nc.vector.scalar_tensor_tensor(out=xb, in0=hb[p], scalar=KEEP, in1=xb, op0=ALU.mult,
                                                                op1=ALU.add))

                    def step(b, j, p, first, more):
                        if more:
                            variance(b + 1)
                        if not second:
                            dve.wait_ge(s_sq, b + 1)
                            nc.vector.tensor_reduce(norm2, qksq, AX.X, ALU.add).then_inc(s_n2, 1)
                        if more:
                            normalise(b + 1, j + p, 1 - p, first and p == 0)
                        if second:
                            dve.wait_ge(s_pr, b + 1)
                            if not first:
                                dve.wait_ge(s_st[p], 16 * stores * j)
                            for f in range(4):
                                last = nc.vector.tensor_copy(
                                    tw[p][:, 2 * f:2 * f + 2, :],
                                    ps[4 + f][:, :].rearrange("p (s c) -> p s c", s=2)[:, :, 0:WA])
                            last.then_inc(s_rows, 1)
                            dve.wait_ge(s_rows, b + 1)
                            nc.vector.tensor_copy(s1_all[:, bass.ts(b, TB)], tw[p][:, :, D + 1])
                            link(nc.vector.tensor_reduce(meanb[:, :], tw[p][:, :, 0:D].rearrange("p s c -> p c s"),
                                                         AX.X, ALU.add))
                            link(nc.vector.tensor_tensor(colsum[:, :], colsum[:, :], meanb[:, :], ALU.add))
                        else:
                            dve.wait_ge(s_nrm, b + 1)
                            link(nc.vector.tensor_scalar(norm, norm, COS_EPS, None, ALU.max))
                            link(nc.vector.reciprocal(norm, norm))
                            if not first:
                                dve.wait_ge(s_st[p], 16 * stores * j)
                            for f in range(4):
                                last = nc.vector.tensor_tensor(
                                    qk[p][:, 2 * f:2 * f + 2, :].rearrange("p s (a c) -> p (s a) c", a=2),
                                    ps[4 + f][:, :].rearrange("p (s c) -> p s c", s=4),
                                    spread(norm[:, 4 * f:4 * f + 4], D), ALU.mult)
                            last.then_inc(s_rows, 1)

                    variance(0)
                    normalise(0, 0, 0, True)
                    steps(dve, link, step)

        table_stage("first", False)

        s_adj = [[sem(f"adj_loaded_{p}{f}") for f in "ab"] for p in range(2)]
        s_cast = [sem(f"adj_cast_{f}") for f in "ab"]
        s_keyu, s_mu = sem("keys_used"), [sem("m16a_folded"), sem("m16b_folded")]
        s_cnt, s_cntT, s_lists = sem("counts"), sem("counts_transposed"), sem("lists_ready")
        s_gate, s_pgate, s_pegate = sem("dve_gate"), sem("l0_pool_gate"), sem("pe_gate")
        s_ch0, s_ipool = sem("l0_dve_chain"), sem("l0_pool_chain")
        s_g = [sem(f"l0_gathered_{p}") for p in range(2)]
        s_own = [sem(f"own_rows_{p}") for p in range(2)]
        s_pm, s_adg = sem("l0_masked"), sem("l0_act_diag")
        s_sc, s_ex, s_dg, s_pv = sem("l0_scores"), sem("l0_exp"), sem("l0_diag"), sem("l0_weighted")
        s_res, s_pvu = sem("l0_rows_done"), sem("l0_pv_used")
        PAIRS = T // 2

        def gathers(pool, p, view, tab, s_got, k):
            for s in range(S):
                def one():
                    pool.indirect_dma_start(
                        out=view[:, s, :], out_offset=None, in_=tab,
                        in_offset=bass.IndirectOffsetOnAxis(ap=idx_st[p][:, s:s + 1], axis=0),
                        bounds_check=N - 1, oob_is_err=False).then_inc(s_got, 16)
                if s < S0:
                    one()
                else:
                    with pool.If(k > s):
                        one()
                    with pool.Else():
                        pool.nop()

        def sized(eng, k, gate, body):
            eng.sem_inc(gate, 1)
            def rest(sizes):
                if len(sizes) == 1:
                    body(sizes[0])
                    return
                with eng.If(k <= sizes[0]):
                    body(sizes[0])
                with eng.Else():
                    rest(sizes[1:])
                    if len(sizes) > 2:
                        eng.nop()
            rest(SIZES)

        def neighbours(eng, t):
            return eng.value_load(kmax_all[0:1, bass.ds(t, 1)], min_val=0, max_val=S)

        with nc.Block() as block:
            @block.sync
            def _(sp):
                def own_rows(i, first):
                    for p in range(2):
                        t = 2 * i + p
                        if not first:
                            sp.wait_ge(s_res, 2 * i + p - 1)
                        sp.dma_start(own[p], kh_t[bass.ds(t, 1)].rearrange("o p c -> (o p) c")).then_inc(s_own[p], 16)

                peel(sp, None, 0, PAIRS, own_rows)

            @block.gpsimd
            def _(pool):
                link = Chain(pool, s_ipool)

                def pair(i, first):
                    pool.wait_ge(s_lists, i + 1)
                    pool.sem_inc(s_pgate, 1)
                    for p in range(2):
                        t = 2 * i + p
                        k = pool.value_load(kmax_all[0:1, bass.ds(t, 1)], min_val=0, max_val=S)
                        if not first:
                            pool.wait_ge(s_pv, 2 * i + p - 1)
                            pool.sem_inc(s_pgate, 1)
                        link(nc.gpsimd.tensor_copy(idx_st[p][:, :], idx_all[:, bass.ts(t, S)]), s_pgate)
                        gathers(pool, p, G0[p], qh_tab, s_g[p], k)

                peel(pool, link, 0, PAIRS, pair)

            @block.scalar
            def _(act):
                def load(t, p, f):
                    lo, hi = ((0, CUT), (CUT, N))[f]
                    act.dma_start(adj_sb[p][f], adj_t[bass.ds(t, 1), :, lo:hi].rearrange(
                        "o p c -> (o p) c")).then_inc(s_adj[p][f], 16)

                def cast(i, p, first=False, more=True):
                    t = 2 * i + p
                    for f in range(2):
                        act.wait_ge(s_adj[p][f], 16 * (i + 1))
                        if not first:
                            act.wait_ge(s_mu[f], t)
                        nc.scalar.activation(m16[f], adj_sb[p][f], ACT.Copy,
                                             accum_out=deg_all[:, bass.ds(2 * t + f, 1)]).then_inc(s_cast[f], 1)
                        if more:
                            act.wait_ge(s_cast[f], t + 1)
                            load(t + 2, p, f)

                def exps(i, p):
                    t = 2 * i + p
                    act.wait_ge(s_sc, t + 1)
                    nc.scalar.activation(prob[:, p, :], score[:, p, :], ACT.Exp).then_inc(s_ex, 1)
                    act.wait_ge(s_pm, t + 1)
                    for s in range(ACT_DIAG):
                        nc.scalar.activation(G0[p][:, s, 0:D], ident[:, :], ACT.Copy, scale=weight[:, p, s:s + 1])
                    nc.scalar.activation(own_diag[p][:, :], ident[:, :], ACT.Copy,
                                         scale=weight[:, p, S:S + 1]).then_inc(s_adg, 1)

                for p in range(2):
                    for f in range(2):
                        load(p, p, f)
                cast(0, 0, first=True)
                cast(0, 1)
                for i in range(2):
                    for p in range(2):
                        cast(i + 1, p)
                with act.Fori(2, PAIRS - 2) as i:
                    for p in range(2):
                        cast(i + 1, p)
                        exps(i - 2, p)
                for p in range(2):
                    cast(PAIRS - 1, p, more=False)
                    exps(PAIRS - 4, p)
                for i in range(PAIRS - 3, PAIRS):
                    for p in range(2):
                        exps(i, p)

            @block.tensor
            def _(pe):
                def folds(i, p, first=False):
                    t = 2 * i + p
                    if not first:
                        pe.wait_ge(s_keyu, t - 1)
                    for h in range(2):
                        o = ps[2 * p + h][:, 0:HW]
                        nc.tensor.matmul(o, ones16[:, :], w_hi[:, h * HW:(h + 1) * HW], start=True, stop=False)
                        nc.tensor.matmul(o, ones16[:, :], w_lo[:, h * HW:(h + 1) * HW], start=False, stop=False)
                    for f, bits in enumerate((range(0, BITS // 2), range(BITS // 2, BITS))):
                        pe.wait_ge(s_cast[f], t + 1)
                        for b in bits:
                            for h in range(2):
                                n = HW if b < BITS - 1 or h == 0 else LAST - HW
                                c = (b - f * (BITS // 2)) * WORDS + h * HW
                                last = nc.tensor.matmul(ps[2 * p + h][:, 0:n], fold[:, b, :], m16[f][:, c:c + n],
                                                        start=False, stop=b == BITS - 1)
                        last.then_inc(s_mu[f], 1)

                def counts(i):
                    pe.wait_ge(s_cnt, i + 1)
                    for p in range(2):
                        last = nc.tensor.matmul(ps[4][0:1, p * P:(p + 1) * P], cnt2[:, p:p + 1], ident[:, :],
                                                start=True, stop=True)
                    last.then_inc(s_cntT, 1)

                def weighted(i, p, first=False):
                    t = 2 * i + p
                    k = neighbours(pe, t)
                    pe.wait_ge(s_dg, t + 1)
                    pe.wait_ge(s_adg, t + 1)
                    if not first:
                        pe.wait_ge(s_res, t - 1)

                    nc.tensor.matmul(ps[5 + p][:, 0:D], own_diag[p][:, :], own[p][:, D:2 * D], start=True, stop=False)

                    def add_up(n):
                        for s in range(n):
                            last = nc.tensor.matmul(ps[5 + p][:, 0:D], G0[p][:, s, 0:D], G0[p][:, s, D:2 * D],
                                                    start=False, stop=s == n - 1)
                        last.then_inc(s_pv, 1)
                    sized(pe, k, s_pegate, add_up)

                folds(0, 0, True)
                folds(0, 1, True)
                for i in range(2):
                    folds(i + 1, 0)
                    folds(i + 1, 1)
                    counts(i)
                def both(i, first, more=True):
                    for p in range(2):
                        if more:
                            folds(i + 1, p)
                        if p == 1:
                            counts(i)
                        weighted(i - 2, p, first)

                peel(pe, None, 2, PAIRS - 1, both)
                both(PAIRS - 1, False, False)
                for i in range(PAIRS - 2, PAIRS):
                    for p in range(2):
                        weighted(i, p)

            @block.vector
            def _(dve):
                link = Chain(dve, s_ch0)

                def extract(i):
                    did = [0, 0]
                    for p in range(2):
                        dve.wait_ge(s_mu[1], 2 * i + p + 1)
                        dve.sem_inc(s_gate, 1)
                        did[p] = link.add(nc.vector.max(top[:, p, 0:8], key_ps[:, 2 * p:2 * p + 2, 0:HW]))
                    for p in range(2):
                        link.wait(did[p], s_gate)
                        nc.vector.match_replace(keys[:, p, :, :], top[:, p, 0:8], key_ps[:, 2 * p:2 * p + 2, 0:HW],
                                                -1.0).then_inc(s_keyu, 1)
                    for p in range(2):
                        dve.wait_ge(s_keyu, 2 * i + p + 1)
                        dve.sem_inc(s_gate, 1)
                        did[p] = link.add(nc.vector.max(top[:, p, 8:16], keys[:, p, :, :]))
                    for p in range(2):
                        link.wait(did[p], s_gate)
                        did[p] = link.add(nc.vector.match_replace(keys[:, p, :, :], top[:, p, 8:16],
                                                                  keys[:, p, :, :], -1.0))
                    for p in range(2):
                        link.wait(did[p], s_gate)
                        did[p] = link.add(nc.vector.max(top[:, p, 16:24], keys[:, p, :, :]))

                def decode(i):
                    link.wait(link.n)
                    link(nc.vector.tensor_copy(keyi[:, :, :], top[:, :, :]))
                    link(nc.vector.tensor_scalar(wi[:, :, :], keyi[:, :, :], (1 << SHIFT) - 1, None, ALU.bitwise_and))
                    sub = link.add(nc.vector.tensor_tensor(left[0], top[:, :, :], wi[:, :, :], ALU.subtract))
                    link.add(nc.vector.tensor_scalar(wpos[:, :, :], wi[:, :, :], float(1 - EXP0 * WORDS), None,
                                                     ALU.add))
                    for r in range(ROUNDS):
                        link.wait(sub)
                        leftb = left[r].bitcast(i32)
                        if r < ROUNDS - 1:
                            bit = link.add(nc.vector.tensor_scalar(tbit[r][:, :, :], leftb, 0x7F800000, None,
                                                                   ALU.bitwise_and))
                        shift = link.add(nc.vector.tensor_scalar(expo[r][:, :, :], leftb, 23, None,
                                                                 ALU.logical_shift_right))
                        if r < ROUNDS - 1:
                            link.wait(bit)
                            sub = link.add(nc.vector.tensor_tensor(left[r + 1], left[r],
                                                                   tbit[r][:, :, :].bitcast(fp32), ALU.subtract))
                        link.wait(shift)
                        link.add(nc.vector.scalar_tensor_tensor(out=cand[:, :, r, :], in0=expo[r][:, :, :],
                                                                scalar=float(WORDS), in1=wpos[:, :, :],
                                                                op0=ALU.mult, op1=ALU.add))
                    did = [link.n, link.n]
                    for r in range(3):
                        for p in range(2):
                            link.wait(did[p], s_gate)
                            did[p] = link.add(nc.vector.max(nbr[:, p, 8 * r:8 * r + 8], cand[:, p, :, :]))
                        for p in range(2):
                            if r < 2:
                                link.wait(did[p], s_gate)
                                did[p] = link.add(nc.vector.match_replace(cand[:, p, :, :], nbr[:, p, 8 * r:8 * r + 8],
                                                                          cand[:, p, :, :], -1e5))
                    flat = nbr[:, :, :].rearrange("p a s -> p (a s)")
                    link.wait(link.n)
                    some = link.add(nc.vector.tensor_scalar(got[:, :], flat, 0.0, None, ALU.is_gt))
                    far = link.add(nc.vector.tensor_scalar(none_at[:, :], flat, 0.0, FAR_IDX, ALU.is_le, ALU.mult))
                    link.wait(some)
                    count = link.add(nc.vector.tensor_reduce(cnt2[:, :], got[:, :].rearrange("p (a s) -> p a s", a=2),
                                                             AX.X, ALU.add))
                    link.wait(far)
                    link.add(nc.vector.scalar_tensor_tensor(out=idx_all[:, bass.ts(i, 2 * S)], in0=flat, scalar=-1.0,
                                                            in1=none_at[:, :], op0=ALU.add, op1=ALU.add))
                    link.wait(count)
                    nc.vector.tensor_copy(cnt_all[:, bass.ts(i, 2)], cnt2[:, :]).then_inc(s_cnt, 1)

                def announce(i):
                    dve.wait_ge(s_cntT, i + 1)
                    kmax = kmax_all[0:1, bass.ts(i, 2)]
                    link(nc.vector.tensor_reduce(kmax, ps[4][0:1, 0:2 * P].rearrange("o (a q) -> o a q", a=2), AX.X, ALU.max))
                    link(nc.vector.tensor_scalar(kput[:, :], kmax, float(S0), 16.0, ALU.max, ALU.mult))
                    link(nc.vector.tensor_tensor(ksum[:, :], ksum[:, :], kput[:, :], ALU.add))
                    nc.vector.tensor_copy(goal_all[0:1, bass.ts(i, 2)], ksum[:, :]).then_inc(s_lists, 1)

                def attend(i, p, first=False):
                    if p == 0:
                        link(nc.vector.tensor_scalar(valid[:, :, :].rearrange("p a s -> p (a s)"),
                                                     idx_all[:, bass.ts(i, 2 * S)], float(NONE), None, ALU.is_lt))
                    t = 2 * i + p
                    q = G0[p][:, :, 0:D]
                    goal = dve.value_load(goal_all[0:1, bass.ds(t, 1)], min_val=16 * S0, max_val=16 * S * T)
                    k = neighbours(dve, t)
                    dve.wait_ge(s_g[p], goal)
                    dve.wait_ge(s_own[p], 16 * (i + 1))

                    def scores(n):
                        link(nc.vector.tensor_tensor(q[:, 0:n, :], q[:, 0:n, :],
                                                     own[p][:, 0:D].unsqueeze(1).to_broadcast([P, n, D]), ALU.mult))
                        nc.vector.tensor_reduce(score[:, p, 0:n], q[:, 0:n, :], AX.X, ALU.add).then_inc(s_sc, 1)
                        if n < S:
                            link.n -= 1
                    sized(dve, k, s_gate, scores)
                    den = st[:, p:p + 1]
                    dve.wait_ge(s_ex, t + 1)
                    link.add(nc.vector.tensor_scalar(weight[:, p, S:S + 1], cnt_all[:, bass.ds(t, 1)], 0.0, None,
                                                     ALU.is_equal))
                    nc.vector.tensor_tensor(weight[:, p, 0:S], prob[:, p, :], valid[:, p, :], ALU.mult).then_inc(s_pm, 1)
                    dve.wait_ge(s_pm, t + 1)

                    def diagonals(n):
                        nc.vector.tensor_tensor(
                            q[:, ACT_DIAG:n, :], ident[:, :].unsqueeze(1).to_broadcast([P, n - ACT_DIAG, D]),
                            spread(weight[:, p, ACT_DIAG:n], D), ALU.mult).then_inc(s_dg, 1)
                    sized(dve, k, s_gate, diagonals)
                    link(nc.vector.tensor_reduce(den, weight[:, p, :], AX.X, ALU.add))
                    link(nc.vector.reciprocal(den, den))
                    if not first:
                        finish(t - 1, 1 - p)

                def row(t):
                    return res[:, bass.ds(t, 1), :].rearrange("p o c -> p (o c)")

                def finish(t, p):
                    dve.wait_ge(s_pv, t + 1)
                    nc.vector.scalar_tensor_tensor(out=row(t), in0=ps[5 + p][:, 0:D], scalar=st[:, p:p + 1],
                                                   in1=row(t), op0=ALU.mult, op1=ALU.add).then_inc(s_res, 1)

                extract(0)
                decode(0)
                announce(0)
                extract(1)
                decode(1)

                def both(i, first):
                    announce(i - 1)
                    extract(i)
                    attend(i - 2, 0, first)
                    decode(i)
                    attend(i - 2, 1)

                peel(dve, link, 2, PAIRS, both)
                announce(PAIRS - 1)
                for i in range(PAIRS - 2, PAIRS):
                    for p in range(2):
                        attend(i, p)
                finish(T - 1, 1)

        s_miss, s_missT, s_flag, s_chf = sem("missed"), sem("missed_transposed"), sem("flag_set"), sem("flag_chain")
        with nc.Block() as block:
            @block.vector
            def _(dve):
                link = Chain(dve, s_chf)
                link(nc.vector.tensor_reduce(s1_all[:, :], deg_all[:, :].rearrange("p (t f) -> p t f", f=2), AX.X,
                                             ALU.add))
                link(nc.vector.tensor_tensor(s1_all[:, :], s1_all[:, :], cnt_all[:, :], ALU.subtract))
                nc.vector.tensor_reduce(st[:, 0:1], s1_all[:, :], AX.X, ALU.max).then_inc(s_miss, 1)
                dve.wait_ge(s_missT, 1)
                nc.vector.tensor_reduce(flag[:, :], ps[0][0:1, 0:P], AX.X, ALU.max).then_inc(s_flag, 1)

            @block.tensor
            def _(pe):
                pe.wait_ge(s_miss, 1)
                nc.tensor.matmul(ps[0][0:1, 0:P], st[:, 0:1], ident[:, :], start=True, stop=True).then_inc(s_missT, 1)

        pos[0] = 0
        wide = take(N)
        adj_d = take(N).bitcast(i32)
        e_d = take(N)
        feat = take(T * D).rearrange("p (t c) -> p t c", t=T)
        own_d, kT, pT = take(2 * D), take(D), [take(512), take(512)]
        C = N // 512

        class Dense:

            def __init__(self, tag, second):
                self.second, self.tab, self.c0 = second, (hw_tab if second else qh_tab), (0 if second else D)
                self.x = sem(f"{tag}_x")
                self.feat = sem(f"{tag}_feat")
                self.row = sem(f"{tag}_row")
                self.wide_ps = sem(f"{tag}_wide_ps")
                self.wide = sem(f"{tag}_wide")
                self.adj = sem(f"{tag}_adj")
                self.own = sem(f"{tag}_own")
                self.k_ps = sem(f"{tag}_k_ps")
                self.kT = sem(f"{tag}_kT")
                self.scores = sem(f"{tag}_scores")
                self.exp = sem(f"{tag}_exp")
                self.masked = sem(f"{tag}_masked")
                self.blocks = sem(f"{tag}_blocks")
                self.blocks_sb = sem(f"{tag}_blocks_sb")
                self.summed = sem(f"{tag}_summed")
                self.rows = sem(f"{tag}_rows")
                self.stored = sem(f"{tag}_stored")
                self.chain = sem(f"{tag}_chain")

            def sync(self, sp):
                if not self.second:
                    x_t = x.rearrange("(t p) c -> p t c", p=P)
                    for b in range(NB):
                        sp.dma_start(res[:, b * TB:(b + 1) * TB, :], x_t[:, b * TB:(b + 1) * TB, :]).then_inc(self.x, 16)
                rows = self.tab.rearrange("(t p) c -> p t c", p=P)
                for b in range(NB):
                    sp.dma_start(feat[:, b * TB:(b + 1) * TB, :],
                                 rows[:, b * TB:(b + 1) * TB, self.c0:self.c0 + D]).then_inc(self.feat, 16)
                if self.second:
                    sp.dma_start(e_d[0:1, :], hw_tab[:, D:D + 1].rearrange("n o -> o n"),
                                 allow_slow_non_contiguous=True).then_inc(self.row, 16)
                else:
                    e_t = e_d.rearrange("p (t c) -> p t c", t=T)
                    for b in range(NB):
                        sp.dma_start(e_t[:, b * TB:(b + 1) * TB, :],
                                     rows[:, b * TB:(b + 1) * TB, 0:D]).then_inc(self.row, 16)

                def tile(t, first):
                    if not first:
                        sp.wait_ge(self.rows, t)
                    sp.dma_start(adj_d, adj_t[bass.ds(t, 1)].rearrange("o p c -> (o p) c")).then_inc(self.adj, 16)
                    if self.second:
                        sp.wait_ge(self.rows, t + 1)
                        sp.dma_start(out_t[bass.ds(t, 1)].rearrange("o p c -> (o p) c"), own_d[:, 0:D]).then_inc(self.stored, 16)
                    else:
                        sp.dma_start(own_d, kh_t[bass.ds(t, 1)].rearrange("o p c -> (o p) c")).then_inc(self.own, 16)
                peel(sp, None, 0, T, tile)
                if self.second:
                    sp.wait_ge(self.stored, 16 * T)

            def tensor(self, pe):
                pe.wait_ge(self.row, 16 if self.second else 16 * NB)
                for c in range(C):
                    if c >= 2:
                        pe.wait_ge(self.wide, c - 1)
                    if self.second:
                        last = nc.tensor.matmul(ps[c % 2][:, :], ones[0:1, :], e_d[0:1, c * 512:(c + 1) * 512],
                                                start=True, stop=True)
                    else:
                        for s in range(4):
                            a = c * 512 + s * P
                            last = nc.tensor.transpose(ps[c % 2][:, s * P:(s + 1) * P], e_d[:, a:a + P], ident[:, :])
                    last.then_inc(self.wide_ps, 1)
                pe.wait_ge(self.wide, C)
                pe.wait_ge(self.feat, 16 * NB)

                def tile(t, first):
                    if not self.second:
                        pe.wait_ge(self.own, 16 * (t + 1))
                        nc.tensor.transpose(ps[7][:, 0:P], own_d[:, 0:D], ident[:, :]).then_inc(self.k_ps, 1)
                        pe.wait_ge(self.kT, t + 1)
                        for c in range(C):
                            if not first or c >= 4:
                                pe.wait_ge(self.exp, C * t + c - 3)
                            nc.tensor.matmul(ps[c % 4][:, :], kT, wide[:, c * 512:(c + 1) * 512], start=True,
                                             stop=True).then_inc(self.scores, 1)
                    if not first:
                        pe.wait_ge(self.rows, t)

                    def add_up(c):
                        pe.wait_ge(self.blocks_sb, C * t + c + 1)
                        for s in range(4):
                            last = nc.tensor.matmul(ps[6][:, 0:D], pT[c % 2][:, s * P:(s + 1) * P],
                                                    feat[:, 4 * c + s, :], start=c == 0 and s == 0,
                                                    stop=c == C - 1 and s == 3)
                        last.then_inc(self.summed, 1)

                    for c in range(C):
                        pe.wait_ge(self.masked, t + 1 if self.second else C * t + c + 1)
                        for s in range(4):
                            a = c * 512 + s * P
                            last = nc.tensor.transpose(ps[4 + c % 2][:, s * P:(s + 1) * P], e_d[:, a:a + P], ident[:, :])
                        last.then_inc(self.blocks, 1)
                        if c >= 1:
                            add_up(c - 1)
                    add_up(C - 1)
                peel(pe, None, 0, T, tile)

            def scalar(self, act):
                def tile(t, first):
                    if self.second:
                        act.wait_ge(self.scores, t + 1)
                        nc.scalar.activation(e_d, e_d, ACT.Exp, bias=st[:, 1:2], accum_out=st[:, 4:5]).then_inc(self.masked, 1)
                    else:
                        for c in range(C):
                            act.wait_ge(self.scores, C * t + c + 1)
                            if not first:
                                act.wait_ge(self.rows, t)
                            nc.scalar.activation(e_d[:, c * 512:(c + 1) * 512], ps[c % 4][:, :],
                                                 ACT.Exp).then_inc(self.exp, 1)
                    for c in range(C):
                        act.wait_ge(self.blocks, C * t + c + 1)
                        if not first or c >= 2:
                            act.wait_ge(self.summed, C * t + c - 1)
                        nc.scalar.copy(pT[c % 2], ps[4 + c % 2][:, :]).then_inc(self.blocks_sb, 1)
                peel(act, None, 0, T, tile)

            def vector(self, dve):
                link = Chain(dve, self.chain)
                for c in range(C):
                    dve.wait_ge(self.wide_ps, c + 1)
                    nc.vector.tensor_copy(wide[:, c * 512:(c + 1) * 512], ps[c % 2][:, :]).then_inc(self.wide, 1)
                if not self.second:
                    dve.wait_ge(self.x, 16 * NB)
                dve.wait_ge(self.wide, C)
                top_s, far, den, none, keep = (st[:, c:c + 1] for c in (0, 1, 4, 5, 6))

                def row(t):
                    return res[:, bass.ds(t, 1), :].rearrange("p o c -> p (o c)")

                def first_layer(t, first):
                    dve.wait_ge(self.k_ps, t + 1)
                    nc.vector.tensor_copy(kT, ps[7][:, 0:P]).then_inc(self.kT, 1)
                    dve.wait_ge(self.adj, 16 * (t + 1))
                    for c in range(C):
                        cols = slice(c * 512, (c + 1) * 512)
                        dve.wait_ge(self.exp, C * t + c + 1)
                        nc.vector.tensor_tensor(e_d[:, cols], e_d[:, cols], adj_d[:, cols], ALU.mult).then_inc(self.masked, 1)
                    dve.wait_ge(self.masked, C * t + C)
                    link(nc.vector.tensor_reduce(den, e_d, AX.X, ALU.add))
                    link(nc.vector.tensor_scalar(none, den, 0.0, None, ALU.is_equal))
                    link(nc.vector.tensor_tensor(den, den, none, ALU.add))
                    link(nc.vector.reciprocal(den, den))
                    link(nc.vector.tensor_scalar(keep, none, KEEP / (1.0 - KEEP), None, ALU.add))
                    link(nc.vector.scalar_tensor_tensor(out=row(t), in0=own_d[:, D:2 * D], scalar=keep, in1=row(t),
                                                        op0=ALU.mult, op1=ALU.add))
                    dve.wait_ge(self.summed, C * t + C)
                    nc.vector.scalar_tensor_tensor(out=row(t), in0=ps[6][:, 0:D], scalar=den, in1=row(t),
                                                   op0=ALU.mult, op1=ALU.add).then_inc(self.rows, 1)

                def second_layer(t, first):
                    s1 = s1_all[:, bass.ds(t, 1)]
                    dve.wait_ge(self.adj, 16 * (t + 1))
                    link(nc.vector.tensor_scalar(e_d, adj_d, -1.0, FAR, ALU.add, ALU.mult))
                    link(nc.vector.tensor_tensor(e_d, e_d, wide, ALU.add))
                    link(nc.vector.tensor_scalar(e_d, e_d, s1, None, ALU.add))
                    link(nc.vector.scalar_tensor_tensor(out=e_d, in0=e_d, scalar=LEAK, in1=e_d, op0=ALU.mult, op1=ALU.max))
                    link(nc.vector.tensor_reduce(top_s, e_d, AX.X, ALU.max))
                    nc.vector.tensor_scalar(far, top_s, -1.0, None, ALU.mult).then_inc(self.scores, 1)
                    dve.wait_ge(self.masked, t + 1)
                    link(nc.vector.reciprocal(den, den))
                    if not first:
                        dve.wait_ge(self.stored, 16 * t)
                    dve.wait_ge(self.summed, C * t + C)
                    nc.vector.scalar_tensor_tensor(out=own_d[:, 0:D], in0=ps[6][:, 0:D], scalar=den, in1=row(t),
                                                   op0=ALU.mult, op1=ALU.add).then_inc(self.rows, 1)
                peel(dve, link, 0, T, second_layer if self.second else first_layer)

        def load_flag(eng):
            return eng.value_load(flag[0:1, 0:1], min_val=0, max_val=N)

        dense0 = Dense("dense0", False)
        with nc.Block() as block:
            def redo(eng, part):
                with eng.If(load_flag(eng) > 0):
                    part(eng)
                with eng.Else():
                    eng.nop()

            @block.sync
            def _(sp):
                redo(sp, dense0.sync)

            @block.tensor
            def _(pe):
                redo(pe, dense0.tensor)

            @block.scalar
            def _(act):
                redo(act, dense0.scalar)

            @block.vector
            def _(dve):
                redo(dve, dense0.vector)

        table_stage("second", True)

        s_cs, s_mean = sem("column_sums"), sem("mean_row")
        s_g1 = [sem(f"l1_gathered_{p}") for p in range(2)]
        s_sc1, s_ex1, s_dg1, s_pv1 = sem("l1_scores"), sem("l1_exp"), sem("l1_diag"), sem("l1_weighted")
        s_rows1, s_out1 = sem("l1_rows"), [sem(f"l1_stored_{p}") for p in range(2)]
        s_ch1, s_pch1, s_pgate1 = sem("l1_dve_chain"), sem("l1_pool_chain"), sem("l1_pool_gate")
        dense1 = Dense("dense1", True)

        def lists_sync(sp):
            def pair(i, first):
                for p in range(2):
                    sp.wait_ge(s_rows1, 2 * i + p + 1)
                    sp.dma_start(out_t[bass.ds(2 * i + p, 1)].rearrange("o p c -> (o p) c"),
                                 outb[p]).then_inc(s_out1[p], 16)
            peel(sp, None, 0, PAIRS, pair)
            for p in range(2):
                sp.wait_ge(s_out1[p], 16 * PAIRS)

        def lists_gpsimd(pool):
            link = Chain(pool, s_pch1)

            def pair(i, first):
                for p in range(2):
                    t = 2 * i + p
                    k = pool.value_load(kmax_all[0:1, bass.ds(t, 1)], min_val=0, max_val=S)
                    if not first:
                        pool.wait_ge(s_pv1, 2 * i + p - 1)
                        pool.sem_inc(s_pgate1, 1)
                    link(nc.gpsimd.tensor_copy(idx_st[p][:, :], idx_all[:, bass.ts(t, S)]), s_pgate1)
                    gathers(pool, p, G1[p], hw_tab, s_g1[p], k)
            peel(pool, link, 0, PAIRS, pair)

        def lists_scalar(act):
            def pair(i, first):
                for p in range(2):
                    act.wait_ge(s_sc1, 2 * i + p + 1)
                    nc.scalar.activation(prob[:, p, :], score[:, p, :], ACT.Exp, bias=st[:, 4 + p:5 + p],
                                         accum_out=st[:, 6 + p:7 + p]).then_inc(s_ex1, 1)
            peel(act, None, 0, PAIRS, pair)

        def lists_tensor(pe):
            pe.wait_ge(s_cs, 1)
            nc.tensor.matmul(ps[7][:, 0:D], ones[:, :], colsum[:, :], start=True, stop=True).then_inc(s_mean, 1)

            def pair(i, first):
                for p in range(2):
                    k = neighbours(pe, 2 * i + p)
                    pe.wait_ge(s_dg1, 2 * i + p + 1)
                    if not first:
                        pe.wait_ge(s_rows1, 2 * i + p - 1)

                    def add_up(n):
                        for s in range(n):
                            last = nc.tensor.matmul(ps[5 + p][:, 0:D], diag1[p][:, s, :], G1[p][:, s, 0:D],
                                                    start=s == 0, stop=s == n - 1)
                        last.then_inc(s_pv1, 1)
                    sized(pe, k, s_pegate, add_up)
            peel(pe, None, 0, PAIRS, pair)

        def lists_vector(dve):
            link = Chain(dve, s_ch1)
            dve.sem_inc(s_cs, 1)
            dve.wait_ge(s_mean, 1)
            link(nc.vector.tensor_scalar(meanb[:, :], ps[7][:, 0:D], 1.0 / N, None, ALU.mult))

            def finish(t, p):
                dve.wait_ge(s_pv1, t + 1)
                nc.vector.scalar_tensor_tensor(out=outb[p], in0=ps[5 + p][:, 0:D], scalar=st[:, 6 + p:7 + p],
                                               in1=outb[p], op0=ALU.mult, op1=ALU.add).then_inc(s_rows1, 1)

            def pair(i, first):
                link(nc.vector.tensor_scalar(valid[:, :, :].rearrange("p a s -> p (a s)"),
                                             idx_all[:, bass.ts(i, 2 * S)], float(NONE), None, ALU.is_lt))
                link(nc.vector.tensor_scalar(negm[:, :, :], valid[:, :, :], -1.0, FAR, ALU.add, ALU.mult))
                for p in range(2):
                    t = 2 * i + p
                    sc, pr, none = score[:, p, :], prob[:, p, :], st[:, 2:3]
                    less, den = st[:, 4 + p:5 + p], st[:, 6 + p:7 + p]
                    goal = dve.value_load(goal_all[0:1, bass.ds(t, 1)], min_val=16 * S0, max_val=16 * S * T)
                    k = neighbours(dve, t)
                    dve.wait_ge(s_g1[p], goal)
                    link(nc.vector.tensor_scalar(sc, G1[p][:, :, D], s1_all[:, bass.ds(t, 1)], None, ALU.add))
                    link(nc.vector.scalar_tensor_tensor(out=sc, in0=sc, scalar=LEAK, in1=sc, op0=ALU.mult, op1=ALU.max))
                    link(nc.vector.tensor_tensor(sc, sc, valid[:, p, :], ALU.mult))
                    link(nc.vector.tensor_tensor(sc, sc, negm[:, p, :], ALU.add))
                    link(nc.vector.tensor_reduce(less, sc, AX.X, ALU.max))
                    nc.vector.tensor_scalar(less, less, -1.0, None, ALU.mult).then_inc(s_sc1, 1)
                    dve.wait_ge(s_ex1, 2 * i + p + 1)

                    def diagonals(n):
                        nc.vector.tensor_tensor(diag1[p][:, 0:n, :], ident[:, :].unsqueeze(1).to_broadcast([P, n, D]),
                                                spread(pr[:, 0:n], D), ALU.mult).then_inc(s_dg1, 1)
                    sized(dve, k, s_gate, diagonals)
                    link(nc.vector.tensor_scalar(none, cnt_all[:, bass.ds(t, 1)], 0.0, None, ALU.is_equal))
                    link(nc.vector.reciprocal(den, den))
                    link(nc.vector.tensor_scalar(st[:, 3:4], none, -1.0, 1.0, ALU.mult, ALU.add))
                    link(nc.vector.tensor_tensor(den, den, st[:, 3:4], ALU.mult))
                    if not first:
                        dve.wait_ge(s_out1[p], 16 * i)
                    link(nc.vector.scalar_tensor_tensor(out=outb[p], in0=meanb[:, :], scalar=none,
                                                        in1=res[:, bass.ds(t, 1), :].rearrange("p o c -> p (o c)"),
                                                        op0=ALU.mult, op1=ALU.add))
                    if not (first and p == 0):
                        finish(t - 1, 1 - p)
            peel(dve, link, 0, PAIRS, pair)
            finish(T - 1, 1)

        with nc.Block() as block:
            def either(eng, dense, lists):
                with eng.If(load_flag(eng) > 0):
                    dense(eng)
                    eng.nop()
                with eng.Else():
                    lists(eng)
                    eng.nop()

            @block.sync
            def _(sp):
                either(sp, dense1.sync, lists_sync)

            @block.gpsimd
            def _(pool):
                either(pool, lambda e: None, lists_gpsimd)

            @block.tensor
            def _(pe):
                either(pe, dense1.tensor, lists_tensor)

            @block.scalar
            def _(act):
                either(act, dense1.scalar, lists_scalar)

            @block.vector
            def _(dve):
                either(dve, dense1.vector, lists_vector)


_INS = ['x', 'adj', 'L0_gnn_Wq', 'L0_gnn_Wk', 'L1_gnn_W', 'L1_gnn_b_W', 'L1_gnn_a_vec', 'L1_gnn_b_a']
_OUTS = [((8192, 128), 'float32')]


def kernel(**inputs):
    import numpy as _np
    import concourse.bacc as _bacc
    from concourse import mybir as _mybir
    from concourse.bass_utils import run_bass_kernel_spmd as _run

    nc = _bacc.Bacc("TRN2", target_bir_lowering=False, num_devices=1)
    arrays, args = {}, []
    for name in _INS:
        a = _np.ascontiguousarray(inputs[name])
        arrays[f"in_{name}_dram"] = a
        args.append(nc.dram_tensor(f"in_{name}_dram", a.shape, _mybir.dt.from_np(a.dtype), kind="ExternalInput").ap())
    for i, (shape, dtype) in enumerate(_OUTS):
        dt = _mybir.dt.from_np(_np.dtype(dtype))
        args.append(nc.dram_tensor(f"out_{i}_dram", shape, dt, kind="ExternalOutput").ap())
    adjacency_layers(nc, *args)
    r = _run(nc, [arrays], core_ids=[0])
    return r.results[0]["out_0_dram"]
```

```python
import concourse.bass as bass
from concourse import mybir
from contextlib import ExitStack


class Chain:

    def __init__(self, eng, sem):
        self.eng, self.sem, self.at, self.n = eng, sem, 0, 0

    def __call__(self, instruction, gate=None):
        self.n += 1
        instruction.then_inc(self.sem, 1)
        self.eng.wait_ge(self.sem, self.at + self.n)
        if gate is not None:
            self.eng.sem_inc(gate, 1)

    def add(self, instruction):
        self.n += 1
        instruction.then_inc(self.sem, 1)
        return self.n

    def wait(self, n, gate=None):
        self.eng.wait_ge(self.sem, self.at + n)
        if gate is not None:
            self.eng.sem_inc(gate, 1)

    def loop(self, i, first, per):
        self.start, self.first, self.per = self.at + self.n, first, per
        self.at, self.n = self.start + (i - first) * per, 0

    def ended(self, end):
        assert self.n == self.per, (self.n, self.per)
        self.at, self.n = self.start + (end - self.first) * self.per, 0


def peel(eng, link, first, end, body):
    before = link.n if link else 0
    body(first, True)
    per = link.n - before if link else 0
    with eng.Fori(first + 1, end) as i:
        if link:
            link.loop(i, first + 1, per)
        body(i, False)
    if link:
        link.ended(end)


def adjacency_layers(nc, x, adj, wq, wk, w, b_w, a_vec, b_a, out):
    fp32, bf16, i32 = mybir.dt.float32, mybir.dt.bfloat16, mybir.dt.int32
    ALU, ACT, AX = mybir.AluOpType, mybir.ActivationFunctionType, mybir.AxisListType

    N, D = x.shape
    P = 128
    T = N // P
    TB = 8
    NB = T // TB
    S = 24
    S0 = 12
    SIZES = [15, 17, 19, S]
    LOADS = 4
    ACT_DIAG = 7
    ROUNDS = 3
    BITS, SHIFT = 14, 10
    WORDS = -(-N // BITS)
    HW = WORDS // 2
    LAST = N - (BITS - 1) * WORDS
    CUT = BITS // 2 * WORDS
    assert WORDS % 2 == 0 and WORDS <= 1 << SHIFT and BITS + SHIFT <= 24
    EXP0 = 127 + SHIFT
    NONE = 8192
    assert N == NONE
    FAR_IDX = float(1 << 20)
    EPS, COS_EPS, LEAK, KEEP = 1e-5, 1e-4, 0.2, 0.5
    FAR = 3e38
    ID, CNT, L = S, S + 1, S + 2
    GROUP = TB * P
    S1 = 2
    WA = D + 2

    qh_tab = nc.dram_tensor("qh_tab", (N, 2 * D), fp32).ap()
    kh_tab = nc.dram_tensor("kh_tab", (N, 2 * D), fp32).ap()
    hw_tab = nc.dram_tensor("hw_tab", (N, WA), fp32).ap()
    own_tab = nc.dram_tensor("own_tab", (N, D + 2), fp32).ap()
    rec_tab = nc.dram_tensor("rec_tab", (N, L), i32).ap()
    own_b = own_tab.rearrange("(b s p) c -> b p s c", p=P, s=TB)
    rec_t = rec_tab.rearrange("(t p) c -> t p c", p=P)
    qh_b = qh_tab.rearrange("(b s p) c -> b p s c", p=P, s=TB)
    kh_b = kh_tab.rearrange("(b s p) c -> b p s c", p=P, s=TB)
    hw_b = hw_tab.rearrange("(b s p) c -> b p s c", p=P, s=TB)
    qh_t = qh_tab.rearrange("(t p) c -> t p c", p=P)
    kh_t = kh_tab.rearrange("(t p) c -> t p c", p=P)
    hw_t = hw_tab.rearrange("(t p) c -> t p c", p=P)
    adj_t = adj.rearrange("(t p) c -> t p c", p=P)
    out_t = out.rearrange("(t p) c -> t p c", p=P)

    ctx = ExitStack()
    with ctx:
        def sb(name, shape, dt=fp32):
            return ctx.enter_context(nc.sbuf_tensor(name, shape, dt))

        def sem(name):
            return ctx.enter_context(nc.semaphore(name))

        ident = sb("ident", [P, P])
        ident16 = sb("ident16", [P, P], bf16)
        ones = sb("ones", [P, P])
        ones16 = sb("ones16", [1, P], bf16)
        fold = sb("fold", [P, BITS, P], bf16)
        w_hi = sb("w_hi", [1, 19 * 32], bf16)
        w_lo = sb("w_lo", [1, 19 * 32], bf16)
        wqkT = sb("wqkT", [P, 2 * D])
        wa = sb("wa", [P, WA])
        ba = sb("ba", [1, WA])
        wraw = sb("wraw", [P, 3 * D])
        avec = sb("avec", [P, 2])
        bcol = sb("bcol", [P, 1])
        brow = sb("brow", [1, D + 1])
        res = sb("res", [P, T, D])
        rec = sb("rec", [P, T, L], i32)
        rec_st = [sb(f"rec_st{q}", [P, L], i32) for q in range(4)]
        key, negkey = sb("key", [P, T]), sb("negkey", [P, T])
        key_lo = sb("key_lo", [P, T])
        place0 = sb("place0", [P, T])
        signs, halfsigns = sb("signs", [P, T]), sb("halfsigns", [P, TB])
        place = sb("place", [P, T], i32)
        cnt_all = sb("cnt_all", [P, T])
        deg_all = sb("deg_all", [P, 2 * T])
        kmax_all = sb("kmax_all", [1, T], i32)
        goal_all = sb("goal_all", [1, T], i32)
        kput = sb("kput", [1, 2])
        ksum = sb("ksum", [1, 2])
        put1, sum1, goal1 = sb("put1", [1, 1]), sb("sum1", [1, 2]), sb("goal1", [1, 2], i32)
        s1_all = sb("s1_all", [P, T])
        colsum = sb("colsum", [P, D])
        meanb = sb("meanb", [P, D])
        flag = sb("flag", [1, 1], i32)
        small = sb("small", [P, 64])

        G_W = S * (WA + D)
        assert G_W >= S * 2 * D

        arena = sb("arena", [P, 2 * N + N // 2 + 16 + 2 * G_W + 4 * D + 4 * (2 * D + 2)])

        pos = [0]

        def take(n):
            n += n % 2
            pos[0] += n
            return arena[:, pos[0] - n:pos[0]]

        def rows_of(n, width=D):
            return take(n * width).rearrange("p (s c) -> p s c", s=n)
        xc, xsq, qksq = rows_of(TB), rows_of(TB), rows_of(2 * TB)
        hb, hh, hT = ([rows_of(TB) for _ in range(2)] for _ in range(3))
        qk = [rows_of(TB, 2 * D) for _ in range(2)]
        tw = [rows_of(TB, WA) for _ in range(2)]
        key_diag, sign_out = rows_of(TB), take(GROUP)
        rec_g = [take(TB * L).bitcast(i32).rearrange("p (s c) -> p s c", s=TB) for _ in range(2)]
        place_g = [take(TB).bitcast(i32) for _ in range(2)]
        pos[0] = 0
        adj_sb = [[take(CUT).bitcast(i32), take(N - CUT).bitcast(i32)] for _ in range(2)]
        m16 = [take(CUT // 2).bitcast(bf16)[:, 0:CUT], take((N - CUT) // 2).bitcast(bf16)[:, 0:N - CUT]]
        G = [take(G_W) for _ in range(2)]
        own = [take(2 * D) for _ in range(2)]
        outb = [take(D) for _ in range(4)]
        own1 = [take(D + 2) for _ in range(4)]
        G0 = [g[:, 0:S * 2 * D].rearrange("p (s c) -> p s c", s=S) for g in G]
        G1 = [g[:, 0:S * WA].rearrange("p (s c) -> p s c", s=S) for g in G]
        diag1 = [g[:, S * WA:S * (WA + D)].rearrange("p (s c) -> p s c", s=S) for g in G]
        idx_st = [sb(f"idx_st{p}", [P, S], i32) for p in range(2)]
        top = sb("top", [P, 2, S])
        keys = sb("keys", [P, 2, 2, HW])
        wpos = sb("wpos", [P, 2, S])
        left = [sb(f"left{r}", [P, 2, S])[:, :, :] for r in range(ROUNDS)]
        got, none_at = sb("got", [P, 2 * S]), sb("none_at", [P, 2 * S])
        keyi, wi = sb("keyi", [P, 2, S], i32), sb("wi", [P, 2, S], i32)
        tbit = [sb(f"tbit{r}", [P, 2, S], i32) for r in range(ROUNDS)]
        expo = [sb(f"expo{r}", [P, 2, S], i32) for r in range(ROUNDS)]
        cnt2 = sb("cnt2", [P, 2])
        cand = sb("cand", [P, 2, ROUNDS, S])
        nbr = sb("nbr", [P, 2, S])
        valid = sb("valid", [P, 2, S])
        score = sb("score", [P, 2, S])
        weight = sb("weight", [P, 2, S + 1])
        own_diag = [sb(f"own_diag{p}", [P, D]) for p in range(2)]
        prob = sb("prob", [P, 2, S])
        negm = sb("negm", [P, 2, S])
        st = sb("st", [P, 32])

        key_ps = ctx.enter_context(nc.psum_tensor("key_ps", [P, 4, 512], fp32))
        ps = [key_ps[:, i, :] for i in range(4)]
        ps += [ctx.enter_context(nc.psum_tensor(f"ps{i}", [P, 512], fp32))[:, :] for i in range(4, 8)]

        s_w, s_x, s_const = sem("weights_loaded"), sem("x_loaded"), sem("constants_made")
        s_wt, s_cpool, s_cdve = sem("weights_transposed"), sem("const_pool_chain"), sem("const_dve_chain")
        with nc.Block() as block:
            @block.sync
            def _(sp):
                sp.dma_start(wraw[:, 0:D], wq).then_inc(s_w, 16)
                sp.dma_start(wraw[:, D:2 * D], wk).then_inc(s_w, 16)
                sp.dma_start(wraw[:, 2 * D:3 * D], w).then_inc(s_w, 16)
                sp.dma_start(avec[:, 0:1], a_vec[D:2 * D].rearrange("(p o) -> p o", o=1)).then_inc(s_w, 16)
                sp.dma_start(avec[:, 1:2], a_vec[0:D].rearrange("(p o) -> p o", o=1)).then_inc(s_w, 16)
                sp.dma_start(bcol[:, :], b_w.rearrange("(p o) -> p o", o=1)).then_inc(s_w, 16)
                sp.dma_start(brow[:, 0:D], b_w.rearrange("(o p) -> o p", o=1)).then_inc(s_w, 16)
                sp.dma_start(brow[:, D:D + 1], b_a.rearrange("(o p) -> o p", o=1)).then_inc(s_w, 16)
                x_t = x.rearrange("(t p) c -> p t c", p=P)
                for b in range(NB):
                    sp.dma_start(res[:, b * TB:(b + 1) * TB, :], x_t[:, b * TB:(b + 1) * TB, :]).then_inc(s_x, 16)
                sp.wait_ge(s_x, 16 * NB)

            @block.gpsimd
            def _(pool):
                link = Chain(pool, s_cpool)
                link(nc.gpsimd.memset(ident[:, :], 0.0))
                link(nc.gpsimd.affine_select(out=ident[:, :], in_=ident[:, :], compare_op=ALU.not_equal,
                                             fill=1.0, base=0, pattern=[[-1, P]], channel_multiplier=1))
                link(nc.gpsimd.memset(ones[:, :], 1.0))
                link(nc.gpsimd.memset(ones16[:, :], 1.0))
                link(nc.gpsimd.iota(key_lo[:, :], [[0, NB], [P, TB]], base=0, channel_multiplier=1,
                                    allow_small_or_imprecise_dtypes=True))
                link(nc.gpsimd.iota(place0[:, :], [[GROUP, NB], [0, TB]], base=GROUP // 2, channel_multiplier=0,
                                    allow_small_or_imprecise_dtypes=True))
                link(nc.gpsimd.iota(place[:, :], [[P, T]], base=0, channel_multiplier=1))
                link(nc.gpsimd.tensor_copy(rec[:, :, ID], place[:, :]))
                link(nc.gpsimd.iota(w_hi[:, :], [[32, 19], [0, 32]], base=0, channel_multiplier=0,
                                    allow_small_or_imprecise_dtypes=True))
                nc.gpsimd.iota(w_lo[:, :], [[0, 19], [1, 32]], base=0, channel_multiplier=0,
                               allow_small_or_imprecise_dtypes=True).then_inc(s_const, 1)
                link(nc.gpsimd.memset(G[1], 0.0))

            @block.tensor
            def _(pe):
                pe.wait_ge(s_w, 128)
                pe.wait_ge(s_const, 1)
                for k in range(3):
                    nc.tensor.transpose(ps[0][:, k * D:(k + 1) * D], wraw[:, k * D:(k + 1) * D], ident[:, :])
                nc.tensor.matmul(ps[1][:, 0:2], wraw[:, 2 * D:3 * D], avec[:, :], start=True, stop=True)
                nc.tensor.matmul(ps[2][0:1, 0:2], bcol[:, :], avec[:, :], start=True,
                                 stop=True).then_inc(s_wt, 1)

            @block.vector
            def _(dve):
                link = Chain(dve, s_cdve)
                link(nc.vector.memset(G[0], 0.0))
                link(nc.vector.memset(colsum[:, :], 0.0))
                link(nc.vector.memset(ksum[:, :], 0.0))
                link(nc.vector.memset(score[:, :, :], 0.0))
                dve.wait_ge(s_const, 1)
                link(nc.vector.tensor_copy(ident16[:, :], ident[:, :]))
                for b in range(BITS):
                    link(nc.vector.tensor_scalar(fold[:, b, :], ident16[:, :], float(1 << (SHIFT + b)), None,
                                                 ALU.mult))
                dve.wait_ge(s_wt, 1)
                dve.wait_ge(s_w, 128)
                link(nc.vector.tensor_copy(wqkT[:, :], ps[0][:, 0:2 * D]))
                link(nc.vector.tensor_copy(wa[:, 0:D], ps[0][:, 2 * D:3 * D]))
                link(nc.vector.tensor_copy(wa[:, D:WA], ps[1][:, 0:2]))
                link(nc.vector.tensor_copy(ba[:, D:WA], ps[2][0:1, 0:2]))
                link(nc.vector.tensor_copy(ba[:, 0:D], brow[:, 0:D]))
                link(nc.vector.tensor_tensor(ba[:, D + 1:WA], ba[:, D + 1:WA], brow[:, D:D + 1], ALU.add))

        def spread(a, n):
            return a.unsqueeze(2).to_broadcast([P, a.shape[1], n])

        def table_stage(tag, second):
            s_var, s_std, s_h = sem(f"{tag}_variance"), sem(f"{tag}_deviation"), sem(f"{tag}_h")
            s_hT, s_hTc, s_pr = sem(f"{tag}_h_transposed"), sem(f"{tag}_hT_copied"), sem(f"{tag}_projected")
            s_sq, s_n2, s_nrm = sem(f"{tag}_squared"), sem(f"{tag}_norm2"), sem(f"{tag}_norm")
            s_rows, s_ch = sem(f"{tag}_rows"), sem(f"{tag}_dve_chain")
            s_st = [sem(f"{tag}_stored_{p}") for p in range(2)]
            stores = 3 if second else 4
            if second:
                s_kd, s_kr, s_sg, s_pl = sem("key_diag"), sem("key_row"), sem("signs"), sem("places")
                s_key, s_rc, s_rs = sem("row_keys"), sem("record_chain"), [sem(f"records_stored_{p}") for p in range(2)]
            mean, inv, var, dev = (st[:, c:c + TB] for c in (0, 8, 16, 24))
            norm2, norm = small[:, 0:16], small[:, 16:32]

            def steps(eng, link, step):
                def two(j, first):
                    for p in range(2):
                        step(2 * j + p, j, p, first, True)
                peel(eng, link, 0, NB // 2 - 1, two)
                step(NB - 2, NB // 2 - 1, 0, False, True)
                step(NB - 1, NB // 2 - 1, 1, False, False)

            with nc.Block() as block:
                @block.sync
                def _(sp):
                    with sp.Fori(0, NB // 2) as j:
                        for p in range(2):
                            b = 2 * j + p
                            sp.wait_ge(s_rows, b + 1)
                            if second:
                                sp.dma_start(hw_b[bass.ds(b, 1)].rearrange("o p s c -> (o p) s c"),
                                             tw[p]).then_inc(s_st[p], 16)
                                sp.dma_start(own_b[bass.ds(b, 1), :, :, 0:D].rearrange("o p s c -> (o p) s c"),
                                             res[:, bass.ts(b, TB), :]).then_inc(s_st[p], 16)
                                sp.dma_start(own_b[bass.ds(b, 1), :, :, D:D + 2].rearrange("o p s c -> (o p) s c"),
                                             tw[p][:, :, D:WA], allow_slow_non_contiguous=True).then_inc(s_st[p], 16)
                                continue
                            for tab, c, rows in ((qh_b, 0, qk[p][:, :, 0:D]), (qh_b, D, hh[p]),
                                                 (kh_b, 0, qk[p][:, :, D:2 * D]), (kh_b, D, hh[p])):
                                sp.dma_start(tab[bass.ds(b, 1), :, :, c:c + D].rearrange("o p s c -> (o p) s c"),
                                             rows).then_inc(s_st[p], 16)
                    for p in range(2):
                        sp.wait_ge(s_st[p], 16 * stores * (NB // 2))

                if second:
                    @block.gpsimd
                    def _(pool):
                        link = Chain(pool, s_rc)

                        def two(j, first):
                            for p in range(2):
                                b = 2 * j + p
                                pool.wait_ge(s_pl, b + 1)
                                if not first:
                                    pool.wait_ge(s_rs[p], 16 * TB * j)
                                link.add(nc.gpsimd.tensor_copy(rec_g[p], rec[:, bass.ts(b, TB), :]))
                                link(nc.gpsimd.tensor_copy(place_g[p], place[:, bass.ts(b, TB)]), s_pgate)
                                for s in range(TB):
                                    pool.indirect_dma_start(
                                        out=rec_tab, out_offset=bass.IndirectOffsetOnAxis(
                                            ap=place_g[p][:, s:s + 1], axis=0),
                                        in_=rec_g[p][:, s, :], in_offset=None,
                                        bounds_check=N - 1, oob_is_err=False).then_inc(s_rs[p], 16)
                        peel(pool, link, 0, NB // 2, two)
                        for p in range(2):
                            pool.wait_ge(s_rs[p], 16 * TB * (NB // 2))

                @block.tensor
                def _(pe):
                    def transposes(b, p):
                        pe.wait_ge(s_h, b + 1)
                        for s in range(TB):
                            last = nc.tensor.transpose(ps[s // 4][:, s % 4 * D:(s % 4 + 1) * D], hb[p][:, s, :],
                                                       ident[:, :])
                        last.then_inc(s_hT, 1)

                    def step(b, j, p, first, more):
                        if second:
                            pe.wait_ge(s_kd, b + 1)
                            if not (first and p == 0):
                                pe.wait_ge(s_sg, TB * b)
                            for f in range(2):
                                last = nc.tensor.matmul(ps[2 + f][:, :], ones[:, :], key_diag[:, 4 * f:4 * f + 4, :],
                                                        start=True, stop=True)
                            last.then_inc(s_kr, 1)
                        pe.wait_ge(s_hTc, b + 1)
                        if not (first and p == 0):
                            pe.wait_ge(s_rows, b)
                        for s in range(TB):
                            o = ps[4 + s // 2][:, s % 2 * 256:s % 2 * 256 + (WA if second else 2 * D)]
                            if second:
                                nc.tensor.matmul(o, hT[p][:, s, :], wa[:, :], start=True, stop=False)
                                last = nc.tensor.matmul(o, ones[0:1, :], ba[:, :], start=False, stop=True)
                            else:
                                last = nc.tensor.matmul(o, hT[p][:, s, :], wqkT[:, :], start=True, stop=True)
                        last.then_inc(s_pr, 1)
                        if more:
                            transposes(b + 1, 1 - p)

                    transposes(0, 0)
                    steps(pe, None, step)

                @block.scalar
                def _(act):
                    def root(b):
                        act.wait_ge(s_var, b + 1)
                        nc.scalar.activation(dev, var, ACT.Sqrt).then_inc(s_std, 1)

                    def copies(b, p):
                        act.wait_ge(s_hT, b + 1)
                        for f in range(2):
                            last = nc.scalar.copy(hT[p][:, 4 * f:4 * f + 4, :],
                                                  ps[f][:, :].rearrange("p (s c) -> p s c", s=4))
                        last.then_inc(s_hTc, 1)

                    def step(b, j, p, first, more):
                        if not second:
                            act.wait_ge(s_pr, b + 1)
                            for f in range(4):
                                last = nc.scalar.activation(qksq[:, 4 * f:4 * f + 4, :],
                                                            ps[4 + f][:, :].rearrange("p (s c) -> p s c", s=4),
                                                            ACT.Square)
                            last.then_inc(s_sq, 1)
                        if more:
                            root(b + 1)
                        if not second:
                            act.wait_ge(s_n2, b + 1)
                            nc.scalar.activation(norm, norm2, ACT.Sqrt).then_inc(s_nrm, 1)
                        if more:
                            copies(b + 1, 1 - p)
                        if second:
                            act.wait_ge(s_kr, b + 1)
                            if first and p == 0:
                                act.wait_ge(s_key, 1)
                            for s in range(TB):
                                at = bass.ds(b * TB + s, 1)
                                if not (first and p == 0 and s == 0):
                                    act.wait_ge(s_sg, b * TB + s)
                                nc.scalar.activation(sign_out.rearrange("p (a c) -> p a c", a=2),
                                                     key_ps[:, 2:4, :], ACT.Sign, bias=negkey[:, at],
                                                     accum_out=signs[:, at]).then_inc(s_sg, 1)

                    root(0)
                    copies(0, 0)
                    steps(act, None, step)

                @block.vector
                def _(dve):
                    link = Chain(dve, s_ch)

                    def variance(b):
                        xb = res[:, bass.ts(b, TB), :]
                        link(nc.vector.tensor_reduce(mean, xb, AX.X, ALU.add))
                        link(nc.vector.tensor_scalar(mean, mean, -1.0 / D, None, ALU.mult))
                        link(nc.vector.tensor_tensor(xc, xb, spread(mean, D), ALU.add))
                        link(nc.vector.tensor_tensor(xsq, xc, xc, ALU.mult))
                        link(nc.vector.tensor_reduce(inv, xsq, AX.X, ALU.add))
                        nc.vector.tensor_scalar(var, inv, 1.0 / D, EPS, ALU.mult, ALU.add).then_inc(s_var, 1)

                    def normalise(b, j, p, first):
                        dve.wait_ge(s_std, b + 1)
                        link(nc.vector.reciprocal(inv, dev))
                        nc.vector.scalar_tensor_tensor(out=hb[p], in0=xc, scalar=0.0, in1=spread(inv, D), op0=ALU.max,
                                                       op1=ALU.mult).then_inc(s_h, 1)
                        if not second:
                            xb = res[:, bass.ts(b, TB), :]
                            dve.wait_ge(s_h, b + 1)
                            if not first:
                                dve.wait_ge(s_st[p], 16 * stores * j)
                            link(nc.vector.tensor_scalar(hh[p], hb[p], 1.0 - KEEP, None, ALU.mult))
                            link(nc.vector.scalar_tensor_tensor(out=xb, in0=hb[p], scalar=KEEP, in1=xb, op0=ALU.mult,
                                                                op1=ALU.add))

                    def key_diagonals(b, first):
                        if not first:
                            dve.wait_ge(s_kr, b)
                        nc.vector.tensor_tensor(key_diag, ident[:, :].unsqueeze(1).to_broadcast([P, TB, D]),
                                                spread(key[:, bass.ts(b, TB)], D), ALU.mult).then_inc(s_kd, 1)

                    def places(b):
                        dve.wait_ge(s_sg, TB * b + TB)
                        link(nc.vector.tensor_scalar(halfsigns[:, :], signs[:, bass.ts(b, TB)], 0.5, None, ALU.mult))
                        nc.vector.scalar_tensor_tensor(
                            out=place[:, bass.ts(b, TB)], in0=halfsigns[:, :], scalar=-0.5,
                            in1=place0[:, bass.ts(b, TB)], op0=ALU.add, op1=ALU.add).then_inc(s_pl, 1)

                    def step(b, j, p, first, more):
                        if second:
                            key_diagonals(b, first and p == 0)
                        if more:
                            variance(b + 1)
                        if not second:
                            dve.wait_ge(s_sq, b + 1)
                            nc.vector.tensor_reduce(norm2, qksq, AX.X, ALU.add).then_inc(s_n2, 1)
                        if more:
                            normalise(b + 1, j + p, 1 - p, first and p == 0)
                        if second:
                            dve.wait_ge(s_pr, b + 1)
                            if not first:
                                dve.wait_ge(s_st[p], 16 * stores * j)
                            for f in range(4):
                                last = nc.vector.tensor_copy(
                                    tw[p][:, 2 * f:2 * f + 2, :],
                                    ps[4 + f][:, :].rearrange("p (s c) -> p s c", s=2)[:, :, 0:WA])
                            last.then_inc(s_rows, 1)
                            dve.wait_ge(s_rows, b + 1)
                            nc.vector.tensor_copy(s1_all[:, bass.ts(b, TB)], tw[p][:, :, D + 1])
                            link(nc.vector.tensor_reduce(meanb[:, :], tw[p][:, :, 0:D].rearrange("p s c -> p c s"),
                                                         AX.X, ALU.add))
                            link(nc.vector.tensor_tensor(colsum[:, :], colsum[:, :], meanb[:, :], ALU.add))
                            if not (first and p == 0):
                                places(b - 1)
                            else:
                                link(nc.vector.memset(halfsigns[:, :], 0.0))
                        else:
                            dve.wait_ge(s_nrm, b + 1)
                            link(nc.vector.tensor_scalar(norm, norm, COS_EPS, None, ALU.max))
                            link(nc.vector.reciprocal(norm, norm))
                            if not first:
                                dve.wait_ge(s_st[p], 16 * stores * j)
                            for f in range(4):
                                last = nc.vector.tensor_tensor(
                                    qk[p][:, 2 * f:2 * f + 2, :].rearrange("p s (a c) -> p (s a) c", a=2),
                                    ps[4 + f][:, :].rearrange("p (s c) -> p s c", s=4),
                                    spread(norm[:, 4 * f:4 * f + 4], D), ALU.mult)
                            last.then_inc(s_rows, 1)

                    if second:
                        link.add(nc.vector.tensor_copy(rec[:, :, CNT], cnt_all[:, :]))
                        link(nc.vector.scalar_tensor_tensor(out=key[:, :], in0=cnt_all[:, :], scalar=float(GROUP),
                                                            in1=key_lo[:, :], op0=ALU.mult, op1=ALU.add))
                        nc.vector.tensor_scalar(negkey[:, :], key[:, :], -1.0, None, ALU.mult).then_inc(s_key, 1)
                    variance(0)
                    normalise(0, 0, 0, True)
                    steps(dve, link, step)
                    if second:
                        dve.wait_ge(s_pl, NB - 1)
                        places(NB - 1)

        table_stage("first", False)

        s_adj = [[[sem(f"adj_loaded_{p}{f}{h}") for h in range(LOADS)] for f in "ab"] for p in range(2)]
        s_cast = [sem(f"adj_cast_{f}") for f in "ab"]
        s_keyu, s_mu = sem("keys_used"), [sem("m16a_folded"), sem("m16b_folded")]
        s_cnt, s_cntT, s_lists = sem("counts"), sem("counts_transposed"), sem("lists_ready")
        s_gate, s_pgate, s_pegate = sem("dve_gate"), sem("l0_pool_gate"), sem("pe_gate")
        s_ch0, s_ipool = sem("l0_dve_chain"), sem("l0_pool_chain")
        s_ga = [sem(f"l0_first_gathered_{p}") for p in range(2)]
        s_g = [sem(f"l0_gathered_{p}") for p in range(2)]
        s_own = [sem(f"own_rows_{p}") for p in range(2)]
        s_pm, s_adg = sem("l0_masked"), sem("l0_act_diag")
        s_sc, s_ex, s_dg, s_pv = sem("l0_scores"), sem("l0_exp"), sem("l0_diag"), sem("l0_weighted")
        s_res, s_pvu = sem("l0_rows_done"), sem("l0_pv_used")
        PAIRS = T // 2

        def gathers(pool, idx, view, tab, s_got, k, always, s_first=None):
            for s in range(S):
                def one():
                    pool.indirect_dma_start(
                        out=view[:, s, :], out_offset=None, in_=tab,
                        in_offset=bass.IndirectOffsetOnAxis(ap=idx[:, s:s + 1], axis=0),
                        bounds_check=N - 1, oob_is_err=False).then_inc(
                            s_first if s_first is not None and s < S0 else s_got, 16)
                if s < always:
                    one()
                else:
                    with pool.If(k > s):
                        one()
                    with pool.Else():
                        pool.nop()

        def sized(eng, k, gate, body, sizes=SIZES):
            eng.sem_inc(gate, 1)
            def rest(sizes):
                if len(sizes) == 1:
                    body(sizes[0])
                    return
                with eng.If(k <= sizes[0]):
                    body(sizes[0])
                with eng.Else():
                    rest(sizes[1:])
                    if len(sizes) > 2:
                        eng.nop()
            rest(sizes)

        def neighbours(eng, t):
            return eng.value_load(kmax_all[0:1, bass.ds(t, 1)], min_val=0, max_val=S)

        with nc.Block() as block:
            @block.sync
            def _(sp):
                def own_rows(i, first):
                    for p in range(2):
                        t = 2 * i + p
                        if not first:
                            sp.wait_ge(s_res, 2 * i + p - 1)
                        sp.dma_start(own[p], kh_t[bass.ds(t, 1)].rearrange("o p c -> (o p) c")).then_inc(s_own[p], 16)

                peel(sp, None, 0, PAIRS, own_rows)

            @block.gpsimd
            def _(pool):
                link = Chain(pool, s_ipool)

                def pair(i, first):
                    pool.wait_ge(s_lists, i + 1)
                    pool.sem_inc(s_pgate, 1)
                    for p in range(2):
                        t = 2 * i + p
                        k = pool.value_load(kmax_all[0:1, bass.ds(t, 1)], min_val=0, max_val=S)
                        if not first:
                            pool.wait_ge(s_pv, 2 * i + p - 1)
                            pool.sem_inc(s_pgate, 1)
                        link(nc.gpsimd.tensor_copy(
                            idx_st[p][:, :], rec[:, bass.ds(t, 1), 0:S].rearrange("p o s -> p (o s)")), s_pgate)
                        gathers(pool, idx_st[p], G0[p], qh_tab, s_g[p], k, S0 + 1, s_ga[p])

                peel(pool, link, 0, PAIRS, pair)

            @block.scalar
            def _(act):
                def load(t, p, f):
                    lo, hi = ((0, CUT), (CUT, N))[f]
                    for h in range(LOADS):
                        a = (hi - lo) * h // LOADS
                        b = (hi - lo) * (h + 1) // LOADS
                        act.dma_start(adj_sb[p][f][:, a:b], adj_t[bass.ds(t, 1), :, lo + a:lo + b].rearrange(
                            "o p c -> (o p) c")).then_inc(s_adj[p][f][h], 16)

                def cast(i, p, first=False, more=True):
                    t = 2 * i + p
                    for f in range(2):
                        for h in range(LOADS):
                            act.wait_ge(s_adj[p][f][h], 16 * (i + 1))
                        if not first:
                            act.wait_ge(s_mu[f], t)
                        nc.scalar.activation(m16[f], adj_sb[p][f], ACT.Copy,
                                             accum_out=deg_all[:, bass.ds(2 * t + f, 1)]).then_inc(s_cast[f], 1)
                        if more:
                            act.wait_ge(s_cast[f], t + 1)
                            load(t + 2, p, f)

                def exps(i, p):
                    t = 2 * i + p
                    act.wait_ge(s_sc, t + 1)
                    nc.scalar.activation(prob[:, p, :], score[:, p, :], ACT.Exp).then_inc(s_ex, 1)
                    act.wait_ge(s_pm, t + 1)
                    for s in range(ACT_DIAG):
                        nc.scalar.activation(G0[p][:, s, 0:D], ident[:, :], ACT.Copy, scale=weight[:, p, s:s + 1])
                    nc.scalar.activation(own_diag[p][:, :], ident[:, :], ACT.Copy,
                                         scale=weight[:, p, S:S + 1]).then_inc(s_adg, 1)

                for p in range(2):
                    for f in range(2):
                        load(p, p, f)
                cast(0, 0, first=True)
                cast(0, 1)
                for i in range(2):
                    for p in range(2):
                        cast(i + 1, p)
                with act.Fori(2, PAIRS - 2) as i:
                    for p in range(2):
                        cast(i + 1, p)
                        exps(i - 2, p)
                for p in range(2):
                    cast(PAIRS - 1, p, more=False)
                    exps(PAIRS - 4, p)
                for i in range(PAIRS - 3, PAIRS):
                    for p in range(2):
                        exps(i, p)

            @block.tensor
            def _(pe):
                def folds(i, p, first=False):
                    t = 2 * i + p
                    if not first:
                        pe.wait_ge(s_keyu, t - 1)
                    for h in range(2):
                        o = ps[2 * p + h][:, 0:HW]
                        nc.tensor.matmul(o, ones16[:, :], w_hi[:, h * HW:(h + 1) * HW], start=True, stop=False)
                        nc.tensor.matmul(o, ones16[:, :], w_lo[:, h * HW:(h + 1) * HW], start=False, stop=False)
                    for f, bits in enumerate((range(0, BITS // 2), range(BITS // 2, BITS))):
                        pe.wait_ge(s_cast[f], t + 1)
                        for b in bits:
                            for h in range(2):
                                n = HW if b < BITS - 1 or h == 0 else LAST - HW
                                c = (b - f * (BITS // 2)) * WORDS + h * HW
                                last = nc.tensor.matmul(ps[2 * p + h][:, 0:n], fold[:, b, :], m16[f][:, c:c + n],
                                                        start=False, stop=b == BITS - 1)
                        last.then_inc(s_mu[f], 1)

                def counts(i):
                    pe.wait_ge(s_cnt, i + 1)
                    for p in range(2):
                        last = nc.tensor.matmul(ps[4][0:1, p * P:(p + 1) * P], cnt2[:, p:p + 1], ident[:, :],
                                                start=True, stop=True)
                    last.then_inc(s_cntT, 1)

                def weighted(i, p, first=False):
                    t = 2 * i + p
                    k = neighbours(pe, t)
                    pe.wait_ge(s_dg, t + 1)
                    pe.wait_ge(s_adg, t + 1)
                    if not first:
                        pe.wait_ge(s_res, t - 1)

                    nc.tensor.matmul(ps[5 + p][:, 0:D], own_diag[p][:, :], own[p][:, D:2 * D], start=True, stop=False)

                    def add_up(n):
                        for s in range(n):
                            last = nc.tensor.matmul(ps[5 + p][:, 0:D], G0[p][:, s, 0:D], G0[p][:, s, D:2 * D],
                                                    start=False, stop=s == n - 1)
                        last.then_inc(s_pv, 1)
                    sized(pe, k, s_pegate, add_up)

                folds(0, 0, True)
                folds(0, 1, True)
                for i in range(2):
                    folds(i + 1, 0)
                    counts(i)
                    folds(i + 1, 1)
                def both(i, first, more=True):
                    for p in range(2):
                        if more:
                            folds(i + 1, p)
                        if p == 1:
                            counts(i)
                        weighted(i - 2, p, first)

                peel(pe, None, 2, PAIRS - 1, both)
                both(PAIRS - 1, False, False)
                for i in range(PAIRS - 2, PAIRS):
                    for p in range(2):
                        weighted(i, p)

            @block.vector
            def _(dve):
                link = Chain(dve, s_ch0)

                def extract(i):
                    did = [0, 0]
                    for p in range(2):
                        dve.wait_ge(s_mu[1], 2 * i + p + 1)
                        dve.sem_inc(s_gate, 1)
                        did[p] = link.add(nc.vector.max(top[:, p, 0:8], key_ps[:, 2 * p:2 * p + 2, 0:HW]))
                    for p in range(2):
                        link.wait(did[p], s_gate)
                        nc.vector.match_replace(keys[:, p, :, :], top[:, p, 0:8], key_ps[:, 2 * p:2 * p + 2, 0:HW],
                                                -1.0).then_inc(s_keyu, 1)
                    for p in range(2):
                        dve.wait_ge(s_keyu, 2 * i + p + 1)
                        dve.sem_inc(s_gate, 1)
                        did[p] = link.add(nc.vector.max(top[:, p, 8:16], keys[:, p, :, :]))
                    for p in range(2):
                        link.wait(did[p], s_gate)
                        did[p] = link.add(nc.vector.match_replace(keys[:, p, :, :], top[:, p, 8:16],
                                                                  keys[:, p, :, :], -1.0))
                    for p in range(2):
                        link.wait(did[p], s_gate)
                        did[p] = link.add(nc.vector.max(top[:, p, 16:24], keys[:, p, :, :]))

                def decode(i):
                    link.wait(link.n)
                    link(nc.vector.tensor_copy(keyi[:, :, :], top[:, :, :]))
                    link(nc.vector.tensor_scalar(wi[:, :, :], keyi[:, :, :], (1 << SHIFT) - 1, None, ALU.bitwise_and))
                    sub = link.add(nc.vector.tensor_tensor(left[0], top[:, :, :], wi[:, :, :], ALU.subtract))
                    link.add(nc.vector.tensor_scalar(wpos[:, :, :], wi[:, :, :], float(1 - EXP0 * WORDS), None,
                                                     ALU.add))
                    for r in range(ROUNDS):
                        link.wait(sub)
                        leftb = left[r].bitcast(i32)
                        if r < ROUNDS - 1:
                            bit = link.add(nc.vector.tensor_scalar(tbit[r][:, :, :], leftb, 0x7F800000, None,
                                                                   ALU.bitwise_and))
                        shift = link.add(nc.vector.tensor_scalar(expo[r][:, :, :], leftb, 23, None,
                                                                 ALU.logical_shift_right))
                        if r < ROUNDS - 1:
                            link.wait(bit)
                            sub = link.add(nc.vector.tensor_tensor(left[r + 1], left[r],
                                                                   tbit[r][:, :, :].bitcast(fp32), ALU.subtract))
                        link.wait(shift)
                        link.add(nc.vector.scalar_tensor_tensor(out=cand[:, :, r, :], in0=expo[r][:, :, :],
                                                                scalar=float(WORDS), in1=wpos[:, :, :],
                                                                op0=ALU.mult, op1=ALU.add))
                    did = [link.n, link.n]
                    for r in range(3):
                        for p in range(2):
                            link.wait(did[p], s_gate)
                            did[p] = link.add(nc.vector.max(nbr[:, p, 8 * r:8 * r + 8], cand[:, p, :, :]))
                        for p in range(2):
                            if r < 2:
                                link.wait(did[p], s_gate)
                                did[p] = link.add(nc.vector.match_replace(cand[:, p, :, :], nbr[:, p, 8 * r:8 * r + 8],
                                                                          cand[:, p, :, :], -1e5))
                    flat = nbr[:, :, :].rearrange("p a s -> p (a s)")
                    link.wait(link.n)
                    some = link.add(nc.vector.tensor_scalar(got[:, :], flat, 0.0, None, ALU.is_gt))
                    far = link.add(nc.vector.tensor_scalar(none_at[:, :], flat, 0.0, FAR_IDX, ALU.is_le, ALU.mult))
                    link.wait(some)
                    count = link.add(nc.vector.tensor_reduce(cnt2[:, :], got[:, :].rearrange("p (a s) -> p a s", a=2),
                                                             AX.X, ALU.add))
                    link.wait(far)
                    link.add(nc.vector.scalar_tensor_tensor(out=rec[:, bass.ts(i, 2), 0:S], in0=nbr[:, :, :],
                                                            scalar=-1.0, op0=ALU.add, op1=ALU.add,
                                                            in1=none_at[:, :].rearrange("p (a s) -> p a s", a=2)))
                    link.wait(count)
                    nc.vector.tensor_copy(cnt_all[:, bass.ts(i, 2)], cnt2[:, :]).then_inc(s_cnt, 1)

                def announce(i):
                    dve.wait_ge(s_cntT, i + 1)
                    kmax = kmax_all[0:1, bass.ts(i, 2)]
                    link(nc.vector.tensor_reduce(kmax, ps[4][0:1, 0:2 * P].rearrange("o (a q) -> o a q", a=2), AX.X, ALU.max))
                    link(nc.vector.tensor_scalar(kput[:, :], kmax, float(S0 + 1), float(-S0), ALU.max, ALU.add))
                    link(nc.vector.scalar_tensor_tensor(out=ksum[:, :], in0=kput[:, :], scalar=16.0, in1=ksum[:, :],
                                                        op0=ALU.mult, op1=ALU.add))
                    nc.vector.tensor_copy(goal_all[0:1, bass.ts(i, 2)], ksum[:, :]).then_inc(s_lists, 1)

                def attend(i, p, first=False):
                    if p == 0:
                        link(nc.vector.tensor_scalar(valid[:, :, :], rec[:, bass.ts(i, 2), 0:S], float(NONE), None,
                                                     ALU.is_lt))
                    t = 2 * i + p
                    q = G0[p][:, :, 0:D]
                    goal = dve.value_load(goal_all[0:1, bass.ds(t, 1)], min_val=16, max_val=16 * S * T)
                    k = neighbours(dve, t)
                    dve.wait_ge(s_own[p], 16 * (i + 1))
                    dve.wait_ge(s_ga[p], 16 * S0 * (i + 1))
                    own_k = own[p][:, 0:D].unsqueeze(1)
                    link(nc.vector.tensor_tensor(q[:, 0:S0, :], q[:, 0:S0, :], own_k.to_broadcast([P, S0, D]), ALU.mult))
                    link.add(nc.vector.tensor_reduce(score[:, p, 0:S0], q[:, 0:S0, :], AX.X, ALU.add))
                    dve.wait_ge(s_g[p], goal)

                    def scores(n):
                        link(nc.vector.tensor_tensor(q[:, S0:n, :], q[:, S0:n, :],
                                                     own_k.to_broadcast([P, n - S0, D]), ALU.mult))
                        nc.vector.tensor_reduce(score[:, p, S0:n], q[:, S0:n, :], AX.X, ALU.add).then_inc(s_sc, 1)
                        if n < S:
                            link.n -= 1
                    sized(dve, k, s_gate, scores)
                    den = st[:, p:p + 1]
                    dve.wait_ge(s_ex, t + 1)
                    link.add(nc.vector.tensor_scalar(weight[:, p, S:S + 1], cnt_all[:, bass.ds(t, 1)], 0.0, None,
                                                     ALU.is_equal))
                    nc.vector.tensor_tensor(weight[:, p, 0:S], prob[:, p, :], valid[:, p, :], ALU.mult).then_inc(s_pm, 1)
                    dve.wait_ge(s_pm, t + 1)

                    def diagonals(n):
                        nc.vector.tensor_tensor(
                            q[:, ACT_DIAG:n, :], ident[:, :].unsqueeze(1).to_broadcast([P, n - ACT_DIAG, D]),
                            spread(weight[:, p, ACT_DIAG:n], D), ALU.mult).then_inc(s_dg, 1)
                    sized(dve, k, s_gate, diagonals)
                    link(nc.vector.tensor_reduce(den, weight[:, p, :], AX.X, ALU.add))
                    link(nc.vector.reciprocal(den, den))
                    if not first:
                        finish(t - 1, 1 - p)

                def row(t):
                    return res[:, bass.ds(t, 1), :].rearrange("p o c -> p (o c)")

                def finish(t, p):
                    dve.wait_ge(s_pv, t + 1)
                    nc.vector.scalar_tensor_tensor(out=row(t), in0=ps[5 + p][:, 0:D], scalar=st[:, p:p + 1],
                                                   in1=row(t), op0=ALU.mult, op1=ALU.add).then_inc(s_res, 1)

                extract(0)
                decode(0)
                announce(0)
                extract(1)
                decode(1)

                def both(i, first):
                    announce(i - 1)
                    extract(i)
                    attend(i - 2, 0, first)
                    decode(i)
                    attend(i - 2, 1)

                peel(dve, link, 2, PAIRS, both)
                announce(PAIRS - 1)
                for i in range(PAIRS - 2, PAIRS):
                    for p in range(2):
                        attend(i, p)
                finish(T - 1, 1)

        s_miss, s_missT, s_flag, s_chf = sem("missed"), sem("missed_transposed"), sem("flag_set"), sem("flag_chain")
        with nc.Block() as block:
            @block.vector
            def _(dve):
                link = Chain(dve, s_chf)
                link(nc.vector.tensor_reduce(s1_all[:, :], deg_all[:, :].rearrange("p (t f) -> p t f", f=2), AX.X,
                                             ALU.add))
                link(nc.vector.tensor_tensor(s1_all[:, :], s1_all[:, :], cnt_all[:, :], ALU.subtract))
                nc.vector.tensor_reduce(st[:, 0:1], s1_all[:, :], AX.X, ALU.max).then_inc(s_miss, 1)
                dve.wait_ge(s_missT, 1)
                nc.vector.tensor_reduce(flag[:, :], ps[0][0:1, 0:P], AX.X, ALU.max).then_inc(s_flag, 1)

            @block.tensor
            def _(pe):
                pe.wait_ge(s_miss, 1)
                nc.tensor.matmul(ps[0][0:1, 0:P], st[:, 0:1], ident[:, :], start=True, stop=True).then_inc(s_missT, 1)

        pos[0] = 0
        wide = take(N)
        adj_d = take(N).bitcast(i32)
        e_d = take(N)
        feat = take(T * D).rearrange("p (t c) -> p t c", t=T)
        own_d, kT, pT = take(2 * D), take(D), [take(512), take(512)]
        C = N // 512

        class Dense:

            def __init__(self, tag, second):
                self.second, self.tab, self.c0 = second, (hw_tab if second else qh_tab), (0 if second else D)
                self.x = sem(f"{tag}_x")
                self.feat = sem(f"{tag}_feat")
                self.row = sem(f"{tag}_row")
                self.wide_ps = sem(f"{tag}_wide_ps")
                self.wide = sem(f"{tag}_wide")
                self.adj = sem(f"{tag}_adj")
                self.own = sem(f"{tag}_own")
                self.k_ps = sem(f"{tag}_k_ps")
                self.kT = sem(f"{tag}_kT")
                self.scores = sem(f"{tag}_scores")
                self.exp = sem(f"{tag}_exp")
                self.masked = sem(f"{tag}_masked")
                self.blocks = sem(f"{tag}_blocks")
                self.blocks_sb = sem(f"{tag}_blocks_sb")
                self.summed = sem(f"{tag}_summed")
                self.rows = sem(f"{tag}_rows")
                self.stored = sem(f"{tag}_stored")
                self.chain = sem(f"{tag}_chain")

            def sync(self, sp):
                if not self.second:
                    x_t = x.rearrange("(t p) c -> p t c", p=P)
                    for b in range(NB):
                        sp.dma_start(res[:, b * TB:(b + 1) * TB, :], x_t[:, b * TB:(b + 1) * TB, :]).then_inc(self.x, 16)
                rows = self.tab.rearrange("(t p) c -> p t c", p=P)
                for b in range(NB):
                    sp.dma_start(feat[:, b * TB:(b + 1) * TB, :],
                                 rows[:, b * TB:(b + 1) * TB, self.c0:self.c0 + D]).then_inc(self.feat, 16)
                if self.second:
                    sp.dma_start(e_d[0:1, :], hw_tab[:, D:D + 1].rearrange("n o -> o n"),
                                 allow_slow_non_contiguous=True).then_inc(self.row, 16)
                else:
                    e_t = e_d.rearrange("p (t c) -> p t c", t=T)
                    for b in range(NB):
                        sp.dma_start(e_t[:, b * TB:(b + 1) * TB, :],
                                     rows[:, b * TB:(b + 1) * TB, 0:D]).then_inc(self.row, 16)

                def tile(t, first):
                    if not first:
                        sp.wait_ge(self.rows, t)
                    sp.dma_start(adj_d, adj_t[bass.ds(t, 1)].rearrange("o p c -> (o p) c")).then_inc(self.adj, 16)
                    if self.second:
                        sp.wait_ge(self.rows, t + 1)
                        sp.dma_start(out_t[bass.ds(t, 1)].rearrange("o p c -> (o p) c"), own_d[:, 0:D]).then_inc(self.stored, 16)
                    else:
                        sp.dma_start(own_d, kh_t[bass.ds(t, 1)].rearrange("o p c -> (o p) c")).then_inc(self.own, 16)
                peel(sp, None, 0, T, tile)
                if self.second:
                    sp.wait_ge(self.stored, 16 * T)

            def tensor(self, pe):
                pe.wait_ge(self.row, 16 if self.second else 16 * NB)
                for c in range(C):
                    if c >= 2:
                        pe.wait_ge(self.wide, c - 1)
                    if self.second:
                        last = nc.tensor.matmul(ps[c % 2][:, :], ones[0:1, :], e_d[0:1, c * 512:(c + 1) * 512],
                                                start=True, stop=True)
                    else:
                        for s in range(4):
                            a = c * 512 + s * P
                            last = nc.tensor.transpose(ps[c % 2][:, s * P:(s + 1) * P], e_d[:, a:a + P], ident[:, :])
                    last.then_inc(self.wide_ps, 1)
                pe.wait_ge(self.wide, C)
                pe.wait_ge(self.feat, 16 * NB)

                def tile(t, first):
                    if not self.second:
                        pe.wait_ge(self.own, 16 * (t + 1))
                        nc.tensor.transpose(ps[7][:, 0:P], own_d[:, 0:D], ident[:, :]).then_inc(self.k_ps, 1)
                        pe.wait_ge(self.kT, t + 1)
                        for c in range(C):
                            if not first or c >= 4:
                                pe.wait_ge(self.exp, C * t + c - 3)
                            nc.tensor.matmul(ps[c % 4][:, :], kT, wide[:, c * 512:(c + 1) * 512], start=True,
                                             stop=True).then_inc(self.scores, 1)
                    if not first:
                        pe.wait_ge(self.rows, t)

                    def add_up(c):
                        pe.wait_ge(self.blocks_sb, C * t + c + 1)
                        for s in range(4):
                            last = nc.tensor.matmul(ps[6][:, 0:D], pT[c % 2][:, s * P:(s + 1) * P],
                                                    feat[:, 4 * c + s, :], start=c == 0 and s == 0,
                                                    stop=c == C - 1 and s == 3)
                        last.then_inc(self.summed, 1)

                    for c in range(C):
                        pe.wait_ge(self.masked, t + 1 if self.second else C * t + c + 1)
                        for s in range(4):
                            a = c * 512 + s * P
                            last = nc.tensor.transpose(ps[4 + c % 2][:, s * P:(s + 1) * P], e_d[:, a:a + P], ident[:, :])
                        last.then_inc(self.blocks, 1)
                        if c >= 1:
                            add_up(c - 1)
                    add_up(C - 1)
                peel(pe, None, 0, T, tile)

            def scalar(self, act):
                def tile(t, first):
                    if self.second:
                        act.wait_ge(self.scores, t + 1)
                        nc.scalar.activation(e_d, e_d, ACT.Exp, bias=st[:, 1:2], accum_out=st[:, 4:5]).then_inc(self.masked, 1)
                    else:
                        for c in range(C):
                            act.wait_ge(self.scores, C * t + c + 1)
                            if not first:
                                act.wait_ge(self.rows, t)
                            nc.scalar.activation(e_d[:, c * 512:(c + 1) * 512], ps[c % 4][:, :],
                                                 ACT.Exp).then_inc(self.exp, 1)
                    for c in range(C):
                        act.wait_ge(self.blocks, C * t + c + 1)
                        if not first or c >= 2:
                            act.wait_ge(self.summed, C * t + c - 1)
                        nc.scalar.copy(pT[c % 2], ps[4 + c % 2][:, :]).then_inc(self.blocks_sb, 1)
                peel(act, None, 0, T, tile)

            def vector(self, dve):
                link = Chain(dve, self.chain)
                for c in range(C):
                    dve.wait_ge(self.wide_ps, c + 1)
                    nc.vector.tensor_copy(wide[:, c * 512:(c + 1) * 512], ps[c % 2][:, :]).then_inc(self.wide, 1)
                if not self.second:
                    dve.wait_ge(self.x, 16 * NB)
                dve.wait_ge(self.wide, C)
                top_s, far, den, none, keep = (st[:, c:c + 1] for c in (0, 1, 4, 5, 6))

                def row(t):
                    return res[:, bass.ds(t, 1), :].rearrange("p o c -> p (o c)")

                def first_layer(t, first):
                    dve.wait_ge(self.k_ps, t + 1)
                    nc.vector.tensor_copy(kT, ps[7][:, 0:P]).then_inc(self.kT, 1)
                    dve.wait_ge(self.adj, 16 * (t + 1))
                    for c in range(C):
                        cols = slice(c * 512, (c + 1) * 512)
                        dve.wait_ge(self.exp, C * t + c + 1)
                        nc.vector.tensor_tensor(e_d[:, cols], e_d[:, cols], adj_d[:, cols], ALU.mult).then_inc(self.masked, 1)
                    dve.wait_ge(self.masked, C * t + C)
                    link(nc.vector.tensor_reduce(den, e_d, AX.X, ALU.add))
                    link(nc.vector.tensor_scalar(none, den, 0.0, None, ALU.is_equal))
                    link(nc.vector.tensor_tensor(den, den, none, ALU.add))
                    link(nc.vector.reciprocal(den, den))
                    link(nc.vector.tensor_scalar(keep, none, KEEP / (1.0 - KEEP), None, ALU.add))
                    link(nc.vector.scalar_tensor_tensor(out=row(t), in0=own_d[:, D:2 * D], scalar=keep, in1=row(t),
                                                        op0=ALU.mult, op1=ALU.add))
                    dve.wait_ge(self.summed, C * t + C)
                    nc.vector.scalar_tensor_tensor(out=row(t), in0=ps[6][:, 0:D], scalar=den, in1=row(t),
                                                   op0=ALU.mult, op1=ALU.add).then_inc(self.rows, 1)

                def second_layer(t, first):
                    s1 = s1_all[:, bass.ds(t, 1)]
                    dve.wait_ge(self.adj, 16 * (t + 1))
                    link(nc.vector.tensor_scalar(e_d, adj_d, -1.0, FAR, ALU.add, ALU.mult))
                    link(nc.vector.tensor_tensor(e_d, e_d, wide, ALU.add))
                    link(nc.vector.tensor_scalar(e_d, e_d, s1, None, ALU.add))
                    link(nc.vector.scalar_tensor_tensor(out=e_d, in0=e_d, scalar=LEAK, in1=e_d, op0=ALU.mult, op1=ALU.max))
                    link(nc.vector.tensor_reduce(top_s, e_d, AX.X, ALU.max))
                    nc.vector.tensor_scalar(far, top_s, -1.0, None, ALU.mult).then_inc(self.scores, 1)
                    dve.wait_ge(self.masked, t + 1)
                    link(nc.vector.reciprocal(den, den))
                    if not first:
                        dve.wait_ge(self.stored, 16 * t)
                    dve.wait_ge(self.summed, C * t + C)
                    nc.vector.scalar_tensor_tensor(out=own_d[:, 0:D], in0=ps[6][:, 0:D], scalar=den, in1=row(t),
                                                   op0=ALU.mult, op1=ALU.add).then_inc(self.rows, 1)
                peel(dve, link, 0, T, second_layer if self.second else first_layer)

        def load_flag(eng):
            return eng.value_load(flag[0:1, 0:1], min_val=0, max_val=N)

        dense0 = Dense("dense0", False)
        with nc.Block() as block:
            def redo(eng, part):
                with eng.If(load_flag(eng) > 0):
                    part(eng)
                with eng.Else():
                    eng.nop()

            @block.sync
            def _(sp):
                redo(sp, dense0.sync)

            @block.tensor
            def _(pe):
                redo(pe, dense0.tensor)

            @block.scalar
            def _(act):
                redo(act, dense0.scalar)

            @block.vector
            def _(dve):
                redo(dve, dense0.vector)

        table_stage("second", True)

        s_cs, s_mean = sem("column_sums"), sem("mean_row")
        s_g1 = [sem(f"l1_gathered_{p}") for p in range(2)]
        s_sc1, s_ex1, s_dg1, s_pv1 = sem("l1_scores"), sem("l1_exp"), sem("l1_diag"), sem("l1_weighted")
        s_rows1, s_out1 = sem("l1_rows"), [sem(f"l1_stored_{q}") for q in range(4)]
        s_rec, s_own1 = ([sem(f"l1_{name}_{q}") for q in range(4)] for name in ("records", "own_rows"))
        s_ch1, s_pch1, s_pgate1 = sem("l1_dve_chain"), sem("l1_pool_chain"), sem("l1_pool_gate")
        dense1 = Dense("dense1", True)

        QUADS = T // 4
        SIZES1 = [6, 8, 10, 12, 16, S]

        def lists_sync(sp):
            def quad(j, first):
                for q in range(4):
                    if not first:
                        sp.wait_ge(s_out1[q], 16 * j)
                    sp.dma_start(rec_st[q][:, :], rec_t[bass.ds(4 * j + q, 1)].rearrange("o p c -> (o p) c")).then_inc(
                        s_rec[q], 16)
            peel(sp, None, 0, QUADS, quad)

        def lists_gpsimd(pool):
            def store(j, q):
                pool.wait_ge(s_rows1, 4 * j + q + 1)
                pool.sem_inc(s_pgate1, 1)
                pool.indirect_dma_start(out=out, out_offset=bass.IndirectOffsetOnAxis(ap=rec_st[q][:, ID:ID + 1], axis=0),
                                        in_=outb[q], in_offset=None, bounds_check=N - 1,
                                        oob_is_err=False).then_inc(s_out1[q], 16)

            def quad(j, first):
                for q in range(4):
                    p = q % 2
                    pool.wait_ge(s_rec[q], 16 * (j + 1))
                    pool.sem_inc(s_pgate1, 1)
                    k = pool.value_load(rec_st[q][0:1, CNT:CNT + 1], min_val=0, max_val=S)
                    if not (first and q < 2):
                        pool.wait_ge(s_pv1, 4 * j + q - 1)
                        pool.sem_inc(s_pgate1, 1)
                    pool.indirect_dma_start(out=own1[q], out_offset=None, in_=own_tab,
                                            in_offset=bass.IndirectOffsetOnAxis(ap=rec_st[q][:, ID:ID + 1], axis=0),
                                            bounds_check=N - 1, oob_is_err=False).then_inc(s_own1[q], 16)
                    gathers(pool, rec_st[q], G1[p], hw_tab, s_g1[p], k, S1)
                    if q >= 2:
                        store(j, q - 2)
                    elif not first:
                        store(j - 1, q + 2)
            peel(pool, None, 0, QUADS, quad)
            for q in (2, 3):
                store(QUADS - 1, q)
            for q in range(4):
                pool.wait_ge(s_out1[q], 16 * QUADS)

        def lists_scalar(act):
            def pair(i, first):
                for p in range(2):
                    act.wait_ge(s_sc1, 2 * i + p + 1)
                    nc.scalar.activation(prob[:, p, :], score[:, p, :], ACT.Exp, bias=st[:, 4 + p:5 + p],
                                         accum_out=st[:, 6 + p:7 + p]).then_inc(s_ex1, 1)
            peel(act, None, 0, PAIRS, pair)

        def lists_tensor(pe):
            pe.wait_ge(s_cs, 1)
            nc.tensor.matmul(ps[7][:, 0:D], ones[:, :], colsum[:, :], start=True, stop=True).then_inc(s_mean, 1)

            def quad(j, first):
                for q in range(4):
                    p = q % 2
                    t = 4 * j + q
                    pe.wait_ge(s_dg1, t + 1)
                    pe.sem_inc(s_pegate, 1)
                    k = pe.value_load(rec_st[q][0:1, CNT:CNT + 1], min_val=0, max_val=S)
                    if not (first and q < 2):
                        pe.wait_ge(s_rows1, t - 1)

                    def add_up(n):
                        for s in range(n):
                            last = nc.tensor.matmul(ps[5 + p][:, 0:D], diag1[p][:, s, :], G1[p][:, s, 0:D],
                                                    start=s == 0, stop=s == n - 1)
                        last.then_inc(s_pv1, 1)
                    sized(pe, k, s_pegate, add_up, SIZES1)
            peel(pe, None, 0, QUADS, quad)

        def lists_vector(dve):
            link = Chain(dve, s_ch1)
            dve.sem_inc(s_cs, 1)
            link(nc.vector.memset(sum1[:, :], 0.0))
            dve.wait_ge(s_mean, 1)
            link(nc.vector.tensor_scalar(meanb[:, :], ps[7][:, 0:D], 1.0 / N, None, ALU.mult))

            def finish(t, q):
                dve.wait_ge(s_pv1, t + 1)
                nc.vector.scalar_tensor_tensor(out=outb[q], in0=ps[5 + q % 2][:, 0:D],
                                               scalar=st[:, 6 + q % 2:7 + q % 2], in1=outb[q], op0=ALU.mult,
                                               op1=ALU.add).then_inc(s_rows1, 1)

            def quad(j, first):
                for q in range(4):
                    p = q % 2
                    t = 4 * j + q
                    sc, pr, none, some = score[:, p, :], prob[:, p, :], st[:, 2:3], st[:, 3:4]
                    less, den = st[:, 4 + p:5 + p], st[:, 6 + p:7 + p]
                    dve.wait_ge(s_rec[q], 16 * (j + 1))
                    count = rec_st[q][0:1, CNT:CNT + 1]
                    link.add(nc.vector.tensor_scalar(valid[:, p, :], rec_st[q][:, 0:S], float(NONE), None, ALU.is_lt))
                    link(nc.vector.tensor_scalar(put1[:, :], count, float(S1), 16.0, ALU.max, ALU.mult))
                    link(nc.vector.tensor_tensor(sum1[:, p:p + 1], sum1[:, p:p + 1], put1[:, :], ALU.add))
                    link(nc.vector.tensor_copy(goal1[:, p:p + 1], sum1[:, p:p + 1]), s_gate)
                    goal = dve.value_load(goal1[0:1, p:p + 1], min_val=16 * S1, max_val=16 * S * T)
                    k = dve.value_load(count, min_val=0, max_val=S)
                    link.add(nc.vector.tensor_scalar(negm[:, p, :], valid[:, p, :], -1.0, FAR, ALU.add, ALU.mult))
                    link(nc.vector.tensor_scalar(none, rec_st[q][:, CNT:CNT + 1], 0.0, None, ALU.is_equal))
                    link.add(nc.vector.tensor_scalar(some, none, -1.0, 1.0, ALU.mult, ALU.add))
                    dve.wait_ge(s_own1[q], 16 * (j + 1))
                    if not first:
                        dve.wait_ge(s_out1[q], 16 * j)
                    link.add(nc.vector.scalar_tensor_tensor(out=outb[q], in0=meanb[:, :], scalar=none,
                                                            in1=own1[q][:, 0:D], op0=ALU.mult, op1=ALU.add))
                    dve.wait_ge(s_g1[p], goal)
                    link(nc.vector.tensor_scalar(sc, G1[p][:, :, D], own1[q][:, D + 1:D + 2], None, ALU.add))
                    link(nc.vector.scalar_tensor_tensor(out=sc, in0=sc, scalar=LEAK, in1=sc, op0=ALU.mult, op1=ALU.max))
                    link(nc.vector.tensor_tensor(sc, sc, valid[:, p, :], ALU.mult))
                    link(nc.vector.tensor_tensor(sc, sc, negm[:, p, :], ALU.add))
                    link(nc.vector.tensor_reduce(less, sc, AX.X, ALU.max))
                    nc.vector.tensor_scalar(less, less, -1.0, None, ALU.mult).then_inc(s_sc1, 1)
                    dve.wait_ge(s_ex1, t + 1)

                    def diagonals(n):
                        nc.vector.tensor_tensor(diag1[p][:, 0:n, :], ident[:, :].unsqueeze(1).to_broadcast([P, n, D]),
                                                spread(pr[:, 0:n], D), ALU.mult).then_inc(s_dg1, 1)
                    sized(dve, k, s_gate, diagonals, SIZES1)
                    link(nc.vector.reciprocal(den, den))
                    link(nc.vector.tensor_tensor(den, den, some, ALU.mult))
                    if not (first and q == 0):
                        finish(t - 1, (q - 1) % 4)
            peel(dve, link, 0, QUADS, quad)
            finish(T - 1, 3)

        with nc.Block() as block:
            def either(eng, dense, lists):
                with eng.If(load_flag(eng) > 0):
                    dense(eng)
                    eng.nop()
                with eng.Else():
                    lists(eng)
                    eng.nop()

            @block.sync
            def _(sp):
                either(sp, dense1.sync, lists_sync)

            @block.gpsimd
            def _(pool):
                either(pool, lambda e: None, lists_gpsimd)

            @block.tensor
            def _(pe):
                either(pe, dense1.tensor, lists_tensor)

            @block.scalar
            def _(act):
                either(act, dense1.scalar, lists_scalar)

            @block.vector
            def _(dve):
                either(dve, dense1.vector, lists_vector)


_INS = ['x', 'adj', 'L0_gnn_Wq', 'L0_gnn_Wk', 'L1_gnn_W', 'L1_gnn_b_W', 'L1_gnn_a_vec', 'L1_gnn_b_a']
_OUTS = [((8192, 128), 'float32')]


def kernel(**inputs):
    import numpy as _np
    import concourse.bacc as _bacc
    from concourse import mybir as _mybir
    from concourse.bass_utils import run_bass_kernel_spmd as _run

    nc = _bacc.Bacc("TRN2", target_bir_lowering=False, num_devices=1)
    arrays, args = {}, []
    for name in _INS:
        a = _np.ascontiguousarray(inputs[name])
        arrays[f"in_{name}_dram"] = a
        args.append(nc.dram_tensor(f"in_{name}_dram", a.shape, _mybir.dt.from_np(a.dtype), kind="ExternalInput").ap())
    for i, (shape, dtype) in enumerate(_OUTS):
        dt = _mybir.dt.from_np(_np.dtype(dtype))
        args.append(nc.dram_tensor(f"out_{i}_dram", shape, dt, kind="ExternalOutput").ap())
    adjacency_layers(nc, *args)
    r = _run(nc, [arrays], core_ids=[0])
    return r.results[0]["out_0_dram"]
```
